# Optimizing a Trainium2 kernel written in Bass

```python
import numpy as np
import jax
import jax.numpy as jnp

def _softmax(x, axis=-1):
    return jax.nn.softmax(x, axis=axis)
def _gelu(x):
    return jax.nn.gelu(x, approximate=True)
def _silu(x):
    return jax.nn.silu(x)
def _sigmoid(x):
    return jax.nn.sigmoid(x)
def _layernorm(x, axis=-1, eps=1e-5):
    m = jnp.mean(x, axis=axis, keepdims=True)
    v = jnp.var(x, axis=axis, keepdims=True)
    return (x - m) / jnp.sqrt(v + eps)
def _scatter_add(tgt, idx, src, axis=0):
    return tgt.at[idx].add(src)
def _segment_sum(src, seg, n):
    return jax.ops.segment_sum(src, seg, n)

kernel_name = 'mk_conv_seq_d2_conv_nchw256_0bc7ab'

def setup_inputs(seed: int = 0):
    np.random.seed(seed)
    _w = jnp.asarray
    def _rec_inputs():
        import jax
        import jax.numpy as jnp
        _gk = jax.random.key(seed)
        x = -0.0002422 + 1 * jax.random.normal(jax.random.fold_in(_gk, 1), (4, 256, 160, 160), jnp.float32)
        return x
    x = _rec_inputs()
    def _L0_conv_setup():
        import jax, jax.numpy as jnp
        import numpy as np
        key = jax.random.key(seed)
        k1, k2, k3, k4 = jax.random.split(key, 4)
        B, C, H, W = (4, 256, 160, 160)
        O = 256
        x = jax.random.normal(k1, (B, C, H, W), dtype=jnp.float32)
        conv_w = jax.random.normal(k2, (O, C), dtype=jnp.float32) / np.sqrt(C).astype(np.float32)
        conv_b = jax.random.normal(k3, (O,), dtype=jnp.float32) * 0.01
        gamma = jax.random.normal(k4, (1,), dtype=jnp.float32) * 0.1
        return {'x': x, 'conv_w': conv_w, 'conv_b': conv_b, 'gamma': gamma}
    _L0_conv_all = _L0_conv_setup()
    _L0_conv_in = {k: v for k, v in _L0_conv_all.items() if k in ('conv_w', 'conv_b', 'gamma', )}
    del _L0_conv_all

    def _L1_conv_setup():
        import jax, jax.numpy as jnp
        import numpy as np
        from jax import lax
        EPS = 1e-05

        def haar_dwt(x):
            B, C, H, W = x.shape
            xr = x.reshape(B, C, H // 2, 2, W // 2, 2)
            a = xr[:, :, :, 0, :, 0]
            b = xr[:, :, :, 0, :, 1]
            c = xr[:, :, :, 1, :, 0]
            d = xr[:, :, :, 1, :, 1]
            ll = (a + b + c + d) * 0.5
            lh = (a + b - c - d) * 0.5
            hl = (a - b + c - d) * 0.5
            hh = (a - b - c + d) * 0.5
            return (ll, lh, hl, hh)

        def haar_idwt(ll, lh, hl, hh):
            B, C, h, w = ll.shape
            a = (ll + lh + hl + hh) * 0.5
            b = (ll + lh - hl - hh) * 0.5
            c = (ll - lh + hl - hh) * 0.5
            d = (ll - lh - hl + hh) * 0.5
            out = jnp.stack([jnp.stack([a, b], axis=-1), jnp.stack([c, d], axis=-1)], axis=-2)
            out = out.transpose(0, 1, 2, 4, 3, 5).reshape(B, C, 2 * h, 2 * w)
            return out

        def conv1x1(x, w, b=None):
            y = jnp.einsum('oc,bchw->bohw', w, x)
            if b is not None:
                y = y + b[None, :, None, None]
            return y

        def bn_eval(x, g, b, m, v):
            inv = g * lax.rsqrt(v + EPS)
            return x * inv[None, :, None, None] + (b - m * inv)[None, :, None, None]
        key = jax.random.key(seed)
        ks = jax.random.split(key, 12)
        B, C, H, W = (8, 256, 160, 160)
        hid = C // 16
        f32 = jnp.float32
        x = jax.random.normal(ks[0], (B, C, H, W), f32)
        fusion_w = jax.random.normal(ks[1], (C, 4 * C), f32) * (1.0 / np.sqrt(4 * C))
        fusion_b = jnp.zeros((C,), f32)
        bn1_g = jnp.ones((C,), f32)
        bn1_b = jnp.zeros((C,), f32)
        bn1_m = jax.random.normal(ks[2], (C,), f32) * 0.1
        bn1_v = jax.random.uniform(ks[3], (C,), f32, 0.5, 1.5)
        sa_w = jax.random.normal(ks[4], (1, 2, 7, 7), f32) * (1.0 / np.sqrt(2 * 49))
        ca_w1 = jax.random.normal(ks[5], (hid, C), f32) * (1.0 / np.sqrt(C))
        ca_w2 = jax.random.normal(ks[6], (C, hid), f32) * (1.0 / np.sqrt(hid))
        proj_w = jax.random.normal(ks[7], (4 * C, C), f32) * (1.0 / np.sqrt(C))
        proj_b = jnp.zeros((4 * C,), f32)
        bn2_g = jnp.ones((4 * C,), f32)
        bn2_b = jnp.zeros((4 * C,), f32)
        bn2_m = jax.random.normal(ks[8], (4 * C,), f32) * 0.1
        bn2_v = jax.random.uniform(ks[9], (4 * C,), f32, 0.5, 1.5)
        return dict(x=x, fusion_w=fusion_w, fusion_b=fusion_b, bn1_g=bn1_g, bn1_b=bn1_b, bn1_m=bn1_m, bn1_v=bn1_v, sa_w=sa_w, ca_w1=ca_w1, ca_w2=ca_w2, proj_w=proj_w, proj_b=proj_b, bn2_g=bn2_g, bn2_b=bn2_b, bn2_m=bn2_m, bn2_v=bn2_v)
    _L1_conv_all = _L1_conv_setup()
    _L1_conv_in = {k: v for k, v in _L1_conv_all.items() if k in ('fusion_w', 'fusion_b', 'bn1_g', 'bn1_b', 'bn1_m', 'bn1_v', 'sa_w', 'ca_w1', 'ca_w2', 'proj_w', 'proj_b', 'bn2_g', 'bn2_b', 'bn2_m', 'bn2_v', )}
    del _L1_conv_all

    return {
        "x": x,
        "L0_conv_conv_w": _L0_conv_in["conv_w"],
        "L0_conv_conv_b": _L0_conv_in["conv_b"],
        "L0_conv_gamma": _L0_conv_in["gamma"],
        "L1_conv_fusion_w": _L1_conv_in["fusion_w"],
        "L1_conv_fusion_b": _L1_conv_in["fusion_b"],
        "L1_conv_bn1_g": _L1_conv_in["bn1_g"],
        "L1_conv_bn1_b": _L1_conv_in["bn1_b"],
        "L1_conv_bn1_m": _L1_conv_in["bn1_m"],
        "L1_conv_bn1_v": _L1_conv_in["bn1_v"],
        "L1_conv_sa_w": _L1_conv_in["sa_w"],
        "L1_conv_ca_w1": _L1_conv_in["ca_w1"],
        "L1_conv_ca_w2": _L1_conv_in["ca_w2"],
        "L1_conv_proj_w": _L1_conv_in["proj_w"],
        "L1_conv_proj_b": _L1_conv_in["proj_b"],
        "L1_conv_bn2_g": _L1_conv_in["bn2_g"],
        "L1_conv_bn2_b": _L1_conv_in["bn2_b"],
        "L1_conv_bn2_m": _L1_conv_in["bn2_m"],
        "L1_conv_bn2_v": _L1_conv_in["bn2_v"],
    }

def reference(x, L0_conv_conv_w, L0_conv_conv_b, L0_conv_gamma, L1_conv_fusion_w, L1_conv_fusion_b, L1_conv_bn1_g, L1_conv_bn1_b, L1_conv_bn1_m, L1_conv_bn1_v, L1_conv_sa_w, L1_conv_ca_w1, L1_conv_ca_w2, L1_conv_proj_w, L1_conv_proj_b, L1_conv_bn2_g, L1_conv_bn2_b, L1_conv_bn2_m, L1_conv_bn2_v):
    import jax
    import jax.numpy as jnp
    def _L0_conv_ref(x, conv_w, conv_b, gamma):
        import jax, jax.numpy as jnp
        import numpy as np
        B, C, H, W = x.shape
        N = H * W
        v = x.reshape(B, C, N)
        key_sm = jax.nn.softmax(v, axis=1)
        q_sm = jax.nn.softmax(v, axis=2)
        vq = jnp.einsum('bcn,bdn->bcd', v, q_sm)
        out = jnp.einsum('bcn,bcd->bnd', key_sm, vq)
        out = out.reshape(B, C, H, W)
        out = gamma * out + x
        y = jnp.einsum('bchw,oc->bohw', out, conv_w) + conv_b[None, :, None, None]
        return y

    def _L1_conv_ref(x, fusion_w, fusion_b, bn1_g, bn1_b, bn1_m, bn1_v, sa_w, ca_w1, ca_w2, proj_w, proj_b, bn2_g, bn2_b, bn2_m, bn2_v):
        import jax, jax.numpy as jnp
        import numpy as np
        from jax import lax
        EPS = 1e-05

        def haar_dwt(x):
            B, C, H, W = x.shape
            xr = x.reshape(B, C, H // 2, 2, W // 2, 2)
            a = xr[:, :, :, 0, :, 0]
            b = xr[:, :, :, 0, :, 1]
            c = xr[:, :, :, 1, :, 0]
            d = xr[:, :, :, 1, :, 1]
            ll = (a + b + c + d) * 0.5
            lh = (a + b - c - d) * 0.5
            hl = (a - b + c - d) * 0.5
            hh = (a - b - c + d) * 0.5
            return (ll, lh, hl, hh)

        def haar_idwt(ll, lh, hl, hh):
            B, C, h, w = ll.shape
            a = (ll + lh + hl + hh) * 0.5
            b = (ll + lh - hl - hh) * 0.5
            c = (ll - lh + hl - hh) * 0.5
            d = (ll - lh - hl + hh) * 0.5
            out = jnp.stack([jnp.stack([a, b], axis=-1), jnp.stack([c, d], axis=-1)], axis=-2)
            out = out.transpose(0, 1, 2, 4, 3, 5).reshape(B, C, 2 * h, 2 * w)
            return out

        def conv1x1(x, w, b=None):
            y = jnp.einsum('oc,bchw->bohw', w, x)
            if b is not None:
                y = y + b[None, :, None, None]
            return y

        def bn_eval(x, g, b, m, v):
            inv = g * lax.rsqrt(v + EPS)
            return x * inv[None, :, None, None] + (b - m * inv)[None, :, None, None]
        identity = x
        ll, lh, hl, hh = haar_dwt(x)
        wav = jnp.concatenate([ll, lh, hl, hh], axis=1)
        fused = jax.nn.relu(bn_eval(conv1x1(wav, fusion_w, fusion_b), bn1_g, bn1_b, bn1_m, bn1_v))
        avg_sp = jnp.mean(fused, axis=1, keepdims=True)
        max_sp = jnp.max(fused, axis=1, keepdims=True)
        sp_in = jnp.concatenate([avg_sp, max_sp], axis=1)
        sp_map = lax.conv_general_dilated(sp_in, sa_w, (1, 1), ((3, 3), (3, 3)), dimension_numbers=('NCHW', 'OIHW', 'NCHW'))
        spatial_out = jax.nn.sigmoid(sp_map) * fused
        avg_ch = jnp.mean(spatial_out, axis=(2, 3), keepdims=True)
        max_ch = jnp.max(spatial_out, axis=(2, 3), keepdims=True)

        def mlp(p):
            return conv1x1(jax.nn.relu(conv1x1(p, ca_w1)), ca_w2)
        ch_map = jax.nn.sigmoid(mlp(avg_ch) + mlp(max_ch))
        channel_out = ch_map * spatial_out
        projected = jax.nn.relu(bn_eval(conv1x1(channel_out, proj_w, proj_b), bn2_g, bn2_b, bn2_m, bn2_v))
        C = projected.shape[1] // 4
        ll_o = projected[:, :C]
        lh_o = projected[:, C:2 * C]
        hl_o = projected[:, 2 * C:3 * C]
        hh_o = projected[:, 3 * C:]
        reconstructed = haar_idwt(ll_o, lh_o, hl_o, hh_o)
        return reconstructed + identity

    def _gn(v, G=32, eps=1e-5):
        B_, C_, H_, W_ = v.shape
        g = v.reshape(B_, G, C_ // G, H_, W_)
        m = jnp.mean(g, axis=(2, 3, 4), keepdims=True)
        s = jnp.var(g, axis=(2, 3, 4), keepdims=True)
        return ((g - m) / jnp.sqrt(s + eps)).reshape(v.shape)

    def _ln_c(v, eps=1e-6):
        m = jnp.mean(v, axis=1, keepdims=True)
        s = jnp.var(v, axis=1, keepdims=True)
        return (v - m) / jnp.sqrt(s + eps)

    def _ln_t(v, eps=1e-5):
        m = jnp.mean(v, axis=-1, keepdims=True)
        s = jnp.var(v, axis=-1, keepdims=True)
        return (v - m) / jnp.sqrt(s + eps)

    def _to_tokens(v):
        B_, C_, H_, W_ = v.shape
        return v.reshape(B_, C_, H_ * W_).transpose(0, 2, 1)
    def _from_tokens(t, like):
        B_, C_, H_, W_ = like.shape
        return t.transpose(0, 2, 1).reshape(B_, C_, H_, W_)

    x = _L0_conv_ref(x, L0_conv_conv_w, L0_conv_conv_b, L0_conv_gamma)
    x = _L1_conv_ref(x, L1_conv_fusion_w, L1_conv_fusion_b, L1_conv_bn1_g, L1_conv_bn1_b, L1_conv_bn1_m, L1_conv_bn1_v, L1_conv_sa_w, L1_conv_ca_w1, L1_conv_ca_w2, L1_conv_proj_w, L1_conv_proj_b, L1_conv_bn2_g, L1_conv_bn2_b, L1_conv_bn2_m, L1_conv_bn2_v)
    return x


_drawn_inputs = setup_inputs


def setup_inputs(seed=0):
    import zlib

    import numpy as np

    out = dict(_drawn_inputs(seed))
    spreads = {'L1_conv_fusion_b': (0.0, 0.286),
     'L1_conv_bn1_g': (1.0, 0.2),
     'L1_conv_bn1_b': (0.0, 0.352),
     'L1_conv_proj_b': (0.0, 0.1),
     'L1_conv_bn2_g': (1.0, 0.2),
     'L1_conv_bn2_b': (0.0, 0.1)}
    factors = {'L0_conv_conv_b': 5.559}
    for name, (base, spread) in spreads.items():
        noise = np.random.default_rng([zlib.crc32(name.encode()), seed]).standard_normal(out[name].shape)
        drawn = base * np.exp(spread * noise) if base else spread * noise
        out[name] = jnp.asarray(drawn.astype(out[name].dtype))
    for name, factor in factors.items():
        out[name] = (out[name] * factor).astype(out[name].dtype)
    return out
```

```python
from contextlib import ExitStack

import numpy as np

import concourse.bass as bass
from concourse import mybir

F32 = mybir.dt.float32
F32R = mybir.dt.float32r
ACT = mybir.ActivationFunctionType
ALU = mybir.AluOpType
AX = mybir.AxisListType

P = 128
C = 256
CT = C // P
H = W = 160
N = H * W
J = N // C
JC = 5
S = J // JC
POS = JC * C
ROWS = POS // W
W2 = W // 2
H2 = H // 2
HR = ROWS // 2
PX = HR * W2
HALF = POS // 2
PXS = H2 * W2
HID = C // 16
KS = 7
PAD = KS // 2
EPS = 1e-5
TILES = JC * CT
VEC = {"conv_b": 0, "fusion_b": 2, "bn1_g": 4, "bn1_b": 6, "bn1_m": 8, "bn1_v": 10,
       "proj_b": 12, "bn2_g": 20, "bn2_b": 28, "bn2_m": 36, "bn2_v": 44}
NVEC = 52


def build(nc, B, x_rows, x_keys, x_pos, conv_w, conv_wT, fusion_wT, proj_wT, w1T, w2T, vectors, gamma, bands,
          identity, out):
    y_dram = nc.dram_tensor("y_scratch", [B, S, P, CT * POS], F32).ap()
    sig_dram = nc.dram_tensor("sig_scratch", [B, H2, W2], F32).ap()

    FQ_READY, VAR_READY, PREP_DONE = [0], [0], [0]

    with ExitStack() as ctx:
        def sb(name, shape, dt=F32, stack=ctx):
            return stack.enter_context(nc.sbuf_tensor(name, shape, dt))

        def sem(name):
            return ctx.enter_context(nc.semaphore(name))

        def sems(name, n):
            return [sem(f"{name}{i}") for i in range(n)]

        ident = sb("ident", [P, P])
        vec = sb("vec", [P, NVEC])
        gam = sb("gam", [P, 1])
        w_hi = sb("w_hi", [P, CT, C], F32R)
        w_lo = sb("w_lo", [P, CT, C], F32R)
        g_hi = sb("g_hi", [P, CT, 4, C], F32R)
        g_lo = sb("g_lo", [P, CT, 4, C], F32R)
        proj = sb("proj", [P, CT, 4 * C])
        w1 = sb("w1", [P, CT, HID])
        w2 = sb("w2", [HID, C])
        band = sb("band", [W2, 2 * KS, W2])
        scale1 = sb("scale1", [P, CT])
        bias1 = sb("bias1", [P, CT])
        scale2 = sb("scale2", [P, 8])
        bias2 = sb("bias2", [P, 8])
        small = sb("small", [P, 16])

        load_ring = [sb(f"load_ring{k}", [P, TILES, C + 1]) for k in range(2)]
        next_ring = [sb(f"next_ring{t}", [P, POS]) for t in range(CT)]
        fused = sb("fused", [P, CT, PXS])
        chunk_max = sb("chunk_max", [P, CT, S])
        chan_max = sb("chan_max", [P, CT])
        m_row = sb("m_row", [P, C])
        key_max = sb("key_max", [P, S, TILES])
        key_max_now = [sb(f"key_max_now{k}", [P, TILES]) for k in range(2)]
        vq_sum = sb("vq_sum", [P, CT])
        vq_scale = sb("vq_scale", [P, CT])
        vqT = sb("vqT", [P, CT, C])
        vq = sb("vq", [P, CT, C + 1])
        attn_inv = sb("attn_inv", [P, CT])
        maps = sb("maps", [W2, 2, H2 + 2 * PAD])
        sig = sb("sig", [H2, W2])
        part_max = sb("part_max", [P, CT, JC])
        part_sum = sb("part_sum", [P, CT, JC])
        stats = sb("stats", [P, CT, 2])
        hidden = sb("hidden", [HID, 2])
        hidden_sum = sb("hidden_sum", [HID, 1])
        chan_gate = sb("chan_gate", [P, CT])

        with ExitStack() as area:
            expo = [sb(f"expo{k}", [P, TILES, C], F32, area) for k in range(2)]
            fT = sb("fT", [P, 4, CT, C], F32, area)
            fq = sb("fq", [P, 4, CT, C], F32, area)
            ftmp = sb("ftmp", [P, 4, CT, C], F32, area)
            wn = sb("wn", [P, CT, C], F32, area)
            wt = sb("wt", [P, CT, C], F32, area)
        with ExitStack() as area:
            out2 = [sb(f"out2_{k}", [P, CT, POS], F32, area) for k in range(2)]
            o_hi = [sb(f"o_hi{k}", [P, CT, POS], F32R, area) for k in range(2)]
            o_lo = [sb(f"o_lo{k}", [P, CT, POS], F32R, area) for k in range(2)]
            y_out = [sb(f"y_out{k}", [P, POS], F32, area) for k in range(CT)]
            fused_now = [sb(f"fused_now{k}", [P, CT, PX], F32, area) for k in range(2)]
        with ExitStack() as area:
            s_hi = [sb(f"s_hi{k}", [P, CT, PX], F32R, area) for k in range(2)]
            s_lo = [sb(f"s_lo{k}", [P, CT, PX], F32R, area) for k in range(2)]
            p_hi = sb("p_hi", [P, CT, 4 * C], F32R, area)
            p_lo = sb("p_lo", [P, CT, 4 * C], F32R, area)
            with ExitStack() as sub:
                sig_all = sb("sig_all", [P, PXS], F32, sub)
                junk = sb("junk", [P, 4 * PX], F32, sub)
            with ExitStack() as sub:
                comp = [sb(f"comp{k}", [P, CT, 4, PX], F32, sub) for k in range(2)]
                pairs = sb("pairs", [P, CT, 4, PX], F32, sub)

        BANK = [ctx.enter_context(nc.psum_tensor(f"bank{i}", [P, 512], F32)) for i in range(8)]
        acc = BANK[0:2]
        conv_bank = BANK[2:4]
        max_bank = BANK[4:7]
        px_bank = BANK[7]

        weights_loaded = sem("weights_loaded")
        first_loaded = sems("first_loaded", 2)
        ring_loaded = sems("ring_loaded", 2)
        pos_loaded = sems("pos_loaded", 2)
        next_loaded = sems("next_loaded", 2)
        sig_loaded = sem("sig_loaded")
        y_stored = sems("y_stored", 2)
        out_stored = sems("out_stored", 2)
        sig_stored = sem("sig_stored")
        prep = sem("prep")
        prep_mm = sem("prep_mm")
        passed = sem("passed")
        prep_root = sem("prep_root")
        first_used = sems("first_used", 2)
        next_used = sems("next_used", 2)
        chan_max_ready = sem("chan_max_ready")
        m_row_done = sem("m_row_done")
        m_row_ready = sem("m_row_ready")
        keymax_ready = sem("keymax_ready")
        shifted = sem("shifted")
        expo_ready = sem("expo_ready")
        rows_used = sems("rows_used", 2)
        vq_steps = sem("vq_steps")
        vq_scaled = sem("vq_scaled")
        vq_turned = sem("vq_turned")
        vq_ready = sem("vq_ready")
        keymax_now = sem("keymax_now")
        spread = sem("spread")
        spread_used = sem("spread_used")
        keys_ready = sem("keys_ready")
        attn_done = sems("attn_done", 2)
        attn_used = sems("attn_used", 2)
        inv_ready = sem("inv_ready")
        hi_ready = sem("hi_ready")
        split_ready = sem("split_ready")
        conv_done = sems("conv_done", 2)
        conv_used = sems("conv_used", 2)
        fused_kept = sem("fused_kept")
        px_done = sem("px_done")
        px_used = sem("px_used")
        maps_ready = sem("maps_ready")
        att_done = sem("att_done")
        att_exp = sem("att_exp")
        att_steps = sem("att_steps")
        sig_ready = sem("sig_ready")
        gated = sem("gated")
        summed = sem("summed")
        stat_steps = sem("stat_steps")
        stats_ready = sem("stats_ready")
        mlp1_done = sem("mlp1_done")
        mlp1_ready = sem("mlp1_ready")
        mlp2_done = sem("mlp2_done")
        gate_exp = sem("gate_exp")
        gate_steps = sem("gate_steps")
        proj_hi_ready = sem("proj_hi_ready")
        proj_ready = sem("proj_ready")
        s_hi_ready = sem("s_hi_ready")
        s_ready = sem("s_ready")
        comp_done = sems("comp_done", 8)
        comp_used = sems("comp_used", 8)
        pairs_ready = sem("pairs_ready")
        haar_ready = sem("haar_ready")
        added = sems("added", 2)

        block = ctx.enter_context(nc.Block())

        def slot(k):
            return load_ring[k][:, :, 0:C]

        def slot4(k):
            return slot(k).rearrange("p (t r) c -> p t r c", t=CT)

        def block_of(tile, t, j):
            return tile[:, t, :].rearrange("p (w n) -> p w n", w=2)[:, :, j * P:(j + 1) * P]

        def parity(tile, t, q):
            half = tile[:, t, q % 2 * HALF:(q % 2 + 1) * HALF]
            return half.rearrange("p (h a w) -> p h a w", a=2, w=W2)[:, :, q // 2, :]

        def at(v, b, s):
            return v[bass.ds(b, 1), bass.ds(s, 1)].rearrange("b s p n -> p (b s n)")

        def at_t(v, b, t, s):
            return at(v, b, s)[:, t * POS:(t + 1) * POS]

        def after(i, k, n):
            return i + (k + n) // 2, (k + n) % 2

        LAST = S // 2 - 1

        def wait_alone(eng, *waits):
            for semaphore, value in waits:
                eng.wait_ge(semaphore, value + (1 if semaphore in FROM_ONE else 0))
            eng.sem_inc(passed, 1)

        FROM_ONE = [keymax_now, split_ready, px_done, px_used, fused_kept, spread_used, summed, s_ready, haar_ready]
        for group in (first_used, next_used, rows_used, attn_done, attn_used, conv_done, conv_used, comp_done,
                      comp_used, added, y_stored, out_stored):
            FROM_ONE += group

        @block.sync
        def _(sp):
            tiled = "(t p) o -> p t o"
            for dst, src in ((ident[:], identity), (vec[:], vectors),
                             (gam[:], gamma.rearrange("(a n) -> a n", a=1).broadcast_to([P, 1])),
                             (fT[:], fusion_wT.rearrange("(q t p) o -> p q t o", q=4, p=P)),
                             (wn[:], conv_w.rearrange(tiled, p=P)), (wt[:], conv_wT.rearrange(tiled, p=P)),
                             (proj[:], proj_wT.rearrange(tiled, p=P)), (w1[:], w1T.rearrange(tiled, p=P)),
                             (w2[:], w2T), (band[:], bands)):
                sp.dma_start(dst, src).then_inc(weights_loaded, 16)

            sp.wait_ge(prep, 1)
            with sp.Fori(0, S // 2) as i:
                for k in range(2):
                    sp.wait_ge(first_used[k], 1 + i)
                    sp.dma_start(slot(k), at(x_pos, 0, 2 * i + k)).then_inc(first_loaded[k], 16)

            with sp.Fori(0, B) as b:
                with sp.Fori(0, S // 2) as i:
                    for k in range(2):
                        wait_alone(sp, (first_used[k], S // 2), (out_stored[k], b * 160), (rows_used[k], b * 10 + i))
                        sp.dma_start(slot(k), at(x_rows, b, 2 * i + k)).then_inc(ring_loaded[k], 16)

                def chunks_before(i, k):
                    return b * 20 if isinstance(i, int) and i == 0 else b * 20 + 2 * i + k - 1

                def load_keys(i, k):
                    sp.wait_ge(attn_done[1], 1 + chunks_before(i, k) * JC)
                    sp.dma_start(slot(k), at(x_keys, b, 2 * i + k)).then_inc(ring_loaded[k], 16)

                def load_pos(i, k):
                    sp.wait_ge(split_ready, 1 + chunks_before(i, k))
                    sp.dma_start(out2[k][:].rearrange("p t n -> p (t n)"), at(x_pos, b, 2 * i + k)).then_inc(pos_loaded[k], 16)

                def load_next(s):
                    for t in range(CT):
                        sp.wait_ge(next_used[t], 1 + b * 20 + s)
                        sp.dma_start(next_ring[t][:], at_t(x_pos, b + 1, t, s)).then_inc(next_loaded[t], 16)

                def store_y(i, k):
                    s = b * 20 + 2 * i + k
                    for t in range(CT):
                        wait_alone(sp, (conv_used[0], s * 5 + 3 + 2 * t), (conv_used[1], s * 5 + 3 + 2 * t))
                        sp.dma_start(at_t(y_dram, b, t, 2 * i + k), y_out[t][:]).then_inc(y_stored[t], 16)

                for k in range(2):
                    sp.wait_ge(rows_used[k], 1 + b * 10 + 10)
                for k in range(2):
                    load_keys(0, k)
                    load_pos(0, k)
                load_next(0)
                with sp.Fori(0, LAST) as i:
                    for k in range(2):
                        load_keys(i + 1, k)
                        load_pos(i + 1, k)
                        store_y(i, k)
                        load_next(2 * i + k + 1)
                load_next(S - 1)
                store_y(LAST, 0)
                store_y(LAST, 1)
                for t in range(CT):
                    sp.wait_ge(y_stored[t], 1 + 320 * b + 320)

                sp.wait_ge(sig_ready, b + 1)
                sp.dma_start(sig_dram[bass.ds(b, 1)].rearrange("b h w -> h (b w)"), sig[:]).then_inc(sig_stored, 16)
                sp.wait_ge(sig_stored, 16 * b + 16)
                sp.dma_start(sig_all[:], sig_dram[bass.ds(b, 1)].rearrange("b h w -> b (h w)").broadcast_to(
                    [P, PXS])).then_inc(sig_loaded, 16)

                def load_y(i, k):
                    sp.dma_start(slot(k), at(y_dram, b, 2 * i + k)).then_inc(ring_loaded[k], 16)

                def store_out(i, k):
                    sp.wait_ge(added[k], 1 + b * 10 + i + 1)
                    sp.dma_start(at(out, b, 2 * i + k), slot(k)).then_inc(out_stored[k], 16)

                for k in range(2):
                    sp.wait_ge(attn_done[1], 1 + (b * 20 + 20) * JC)
                    load_y(0, k)
                with sp.Fori(0, LAST) as i:
                    for k in range(2):
                        store_out(i, k)
                        sp.wait_ge(out_stored[k], 1 + 160 * b + 16 * i + 16)
                        load_y(i + 1, k)
                for k in range(2):
                    store_out(LAST, k)
            for k in range(2):
                sp.wait_ge(out_stored[k], 1 + 160 * B)

        @block.vector
        def _(dve):
            steps = [0]

            def step(ins):
                steps[0] += 1
                ins.then_inc(prep, 1)
                dve.wait_ge(prep, steps[0])

            def col(name, n=CT):
                return vec[:, VEC[name]:VEC[name] + n]

            dve.memset(vq[:, :, C:C + 1], 1.0)
            dve.memset(load_ring[0][:, :, C:C + 1], 1.0)
            dve.memset(load_ring[1][:, :, C:C + 1], 1.0)
            step(dve.memset(maps[:], 0.0))
            dve.wait_ge(weights_loaded, 160)
            step(dve.tensor_tensor(ftmp[:, 0:2], fT[:, 0:3:2], fT[:, 1:4:2], ALU.add))
            step(dve.tensor_tensor(ftmp[:, 2:4], fT[:, 0:3:2], fT[:, 1:4:2], ALU.subtract))
            for n in range(2):
                step(dve.tensor_tensor(fq[:, 2 * n], ftmp[:, 2 * n], ftmp[:, 2 * n + 1], ALU.add))
                step(dve.tensor_tensor(fq[:, 2 * n + 1], ftmp[:, 2 * n], ftmp[:, 2 * n + 1], ALU.subtract))
            FQ_READY[0] = steps[0]
            step(dve.tensor_scalar(small[:, 0:2], col("bn1_v"), EPS, None, ALU.add))
            step(dve.tensor_scalar(small[:, 2:10], col("bn2_v", 8), EPS, None, ALU.add))
            VAR_READY[0] = steps[0]
            step(dve.tensor_copy(w_hi[:], wt[:]))
            step(dve.tensor_tensor(w_lo[:], wt[:], w_hi[:].bitcast(F32), ALU.subtract))
            dve.wait_ge(prep_root, 1)
            step(dve.reciprocal(small[:, 0:10], small[:, 0:10]))
            step(dve.tensor_tensor(scale1[:], small[:, 0:2], col("bn1_g"), ALU.mult))
            step(dve.tensor_tensor(scale2[:], small[:, 2:10], col("bn2_g", 8), ALU.mult))
            for n in range(4):
                t, q = n // 2, n % 2 * 2
                dve.wait_ge(prep_mm, n + 1)
                src = BANK[n][:].rearrange("p (q o) -> p q o", q=2)
                step(dve.tensor_copy(g_hi[:, t, q:q + 2, :], src))
                step(dve.tensor_tensor(g_lo[:, t, q:q + 2, :], src, g_hi[:, t, q:q + 2, :].bitcast(F32), ALU.subtract))
            dve.wait_ge(prep_mm, 6)
            for t in range(CT):
                step(dve.tensor_scalar(small[:, 10 + t:11 + t], BANK[4 + t][:, 0:1], 0.5, None, ALU.mult))
            step(dve.tensor_tensor(bias1[:], small[:, 10:12], col("fusion_b"), ALU.add))
            step(dve.tensor_tensor(bias1[:], bias1[:], col("bn1_m"), ALU.subtract))
            step(dve.tensor_tensor(bias1[:], bias1[:], scale1[:], ALU.mult))
            step(dve.tensor_tensor(bias1[:], bias1[:], col("bn1_b"), ALU.add))
            step(dve.tensor_scalar(scale1[:], scale1[:], 0.5, None, ALU.mult))
            step(dve.tensor_tensor(bias2[:], col("proj_b", 8), col("bn2_m", 8), ALU.subtract))
            step(dve.tensor_tensor(bias2[:], bias2[:], scale2[:], ALU.mult))
            step(dve.tensor_tensor(bias2[:], bias2[:], col("bn2_b", 8), ALU.add))
            step(dve.tensor_scalar(bias2[:], bias2[:], 0.5, None, ALU.mult))
            step(dve.tensor_scalar(scale2[:], scale2[:], 0.5, None, ALU.mult))
            PREP_DONE[0] = steps[0]

            with dve.Fori(0, S // 2) as i:
                for k in range(2):
                    dve.wait_ge(first_loaded[k], (i + 1) * 16)
                    for t in range(CT):
                        last = dve.tensor_reduce(chunk_max[:, t, bass.ds(2 * i + k, 1)], slot4(k)[:, t], AX.XY, ALU.max)
                    last.then_inc(first_used[k], 1)

            with dve.Fori(0, B) as b:
                for t in range(CT):
                    dve.wait_ge(first_used[t], 1 + S // 2)
                    dve.wait_ge(next_used[t], 1 + 20 * b)
                dve.tensor_reduce(chan_max[:], chunk_max[:], AX.X, ALU.max).then_inc(chan_max_ready, 1)
                dve.wait_ge(m_row_done, b + 1)
                dve.tensor_copy(m_row[:], max_bank[0][:, 0:C]).then_inc(m_row_ready, 1)
                dve.wait_ge(m_row_ready, b + 1)

                wait_alone(dve, (added[0], 10 * b), (added[1], 10 * b), (comp_done[7], 20 * b), (keymax_now, 20 * b))
                with dve.Fori(0, S // 2) as i:
                    for k in range(2):
                        dve.wait_ge(ring_loaded[k], (b * 30 + i + 1) * 16)
                        dve.tensor_reduce(key_max[:, bass.ds(2 * i + k, 1), :].rearrange("p s t -> p (s t)"), slot(k),
                                          AX.X, ALU.max).then_inc(keymax_ready, 1)
                        dve.wait_ge(rows_used[k], 1 + b * 10 + i)
                        dve.tensor_tensor(expo[k][:], slot(k), m_row[:].rearrange("p (a c) -> p a c", a=1).broadcast_to(
                            [P, TILES, C]), ALU.subtract).then_inc(shifted, 1)

                for k in range(2):
                    dve.wait_ge(rows_used[k], 1 + b * 10 + 10)
                for t in range(CT):
                    dve.reciprocal(vq_sum[:, t:t + 1], acc[t][:, C:C + 1]).then_inc(vq_steps, 1)
                dve.wait_ge(vq_steps, 3 * b + 2)
                dve.tensor_scalar(vq_scale[:], vq_sum[:], gam[:, 0:1], None, ALU.mult).then_inc(vq_steps, 1)
                dve.wait_ge(vq_steps, 3 * b + 3)
                for t in range(CT):
                    dve.tensor_scalar(vqT[:, t, :], acc[t][:, 0:C], vq_scale[:, t:t + 1], None, ALU.mult).then_inc(
                        vq_scaled, 1)
                dve.wait_ge(vq_turned, b + 1)
                for t in range(CT):
                    dve.tensor_copy(vq[:, t, 0:C].rearrange("p (w n) -> p w n", w=2),
                                    conv_bank[t][:, 0:C].rearrange("p (n w) -> p w n", w=2)).then_inc(vq_ready, 1)

                def shift_keys(i, k):
                    s = b * 20 + 2 * i + k
                    dve.wait_ge(ring_loaded[k], (b * 30 + 10 + i + 1) * 16)
                    for n in range(3):
                        dve.wait_ge(spread, s * 3 + n + 1)
                        r = min(2, JC - 2 * n)
                        piece = slot4(k)[:, :, 2 * n:2 * n + r, :]
                        dve.tensor_tensor(piece, piece, max_bank[n][:, 0:r * C].rearrange(
                            "p (a r c) -> p a r c", a=1, c=C).broadcast_to([P, CT, r, C]),
                            ALU.subtract).then_inc(spread_used, 1)

                def add_attention(i, k):
                    s = b * 20 + 2 * i + k
                    dve.wait_ge(pos_loaded[k], (b * 10 + i + 1) * 16)
                    for j in range(JC):
                        for t in range(CT):
                            dve.wait_ge(attn_done[t], 1 + s * JC + j + 1)
                            dve.reciprocal(attn_inv[:, t:t + 1], acc[t][:, C:C + 1]).then_inc(inv_ready, 1)
                            dve.wait_ge(inv_ready, (s * JC + j) * CT + t + 1)
                            o = block_of(out2[k], t, j)
                            dve.scalar_tensor_tensor(out=o, in0=acc[t][:, 0:C].rearrange("p (w n) -> p w n", w=2),
                                                     scalar=attn_inv[:, t:t + 1], in1=o, op0=ALU.mult,
                                                     op1=ALU.add).then_inc(attn_used[t], 1)

                def split(i, k):
                    s = b * 20 + 2 * i + k
                    for t in range(CT):
                        dve.wait_ge(attn_used[t], 1 + (s + 1) * JC)
                    dve.wait_ge(conv_done[1], 1 + ((b * 20 if isinstance(i, int) and i == 0 else s - 1) * 5))
                    dve.tensor_copy(o_hi[k][:], out2[k][:]).then_inc(hi_ready, 1)
                    dve.wait_ge(hi_ready, s + 1)
                    dve.tensor_tensor(o_lo[k][:], out2[k][:], o_hi[k][:].bitcast(F32), ALU.subtract).then_inc(
                        split_ready, 1)

                def map_rows(i, k, n):
                    s = b * 20 + 2 * i + k
                    dve.wait_ge(px_done, 1 + 2 * s + n + 1)
                    src = px_bank[0:W2, :].rearrange("p (r c) -> p r c", c=C)
                    at_row = (2 * i + k) * HR + 2 * n + PAD
                    dve.tensor_reduce(maps[:, 1, bass.ds(at_row, 2)], src, AX.X, ALU.max)
                    dve.tensor_reduce(maps[:, 0, bass.ds(at_row, 2)], src, AX.X, ALU.add).then_inc(px_used, 1)

                def next_maxima(s):
                    for t in range(CT):
                        dve.wait_ge(next_loaded[t], (b * 20 + s + 1) * 16)
                        dve.tensor_reduce(chunk_max[:, t, bass.ds(s, 1)], next_ring[t][:], AX.X, ALU.max).then_inc(
                            next_used[t], 1)

                def rest(i, k):
                    map_rows(i, k, 0)
                    next_maxima(2 * i + k)
                    map_rows(i, k, 1)

                shift_keys(0, 0)
                add_attention(0, 0)
                shift_keys(0, 1)
                split(0, 0)
                with dve.Fori(0, LAST) as i:
                    for k in range(2):
                        add_attention(*after(i, k, 1))
                        shift_keys(i + 1, k)
                        split(*after(i, k, 1))
                        rest(i, k)
                add_attention(LAST, 1)
                split(LAST, 1)
                rest(LAST, 0)
                rest(LAST, 1)

                dve.wait_ge(px_used, 1 + 40 * b + 40)
                dve.tensor_scalar(maps[:, 0, PAD:PAD + H2], maps[:, 0, PAD:PAD + H2], 1.0 / C, None, ALU.mult).then_inc(
                    maps_ready, 1)
                dve.wait_ge(att_exp, b + 1)
                dve.tensor_scalar(sig[:], sig[:], 1.0, None, ALU.add).then_inc(att_steps, 1)
                dve.wait_ge(att_steps, b + 1)
                dve.reciprocal(sig[:], sig[:]).then_inc(sig_ready, 1)
                wait_alone(dve, (sig_loaded, 16 * b + 16), (fused_kept, 20 * b + 20))
                n = PXS // JC
                for q in range(JC):
                    for t in range(CT):
                        f = fused[:, t, q * n:(q + 1) * n]
                        dve.tensor_tensor_reduce(f, f, sig_all[:, q * n:(q + 1) * n], 1.0, 0.0, ALU.mult, ALU.max,
                                                 part_max[:, t, q:q + 1]).then_inc(gated, 1)
                dve.wait_ge(gated, 10 * b + 10)
                dve.tensor_reduce(stats[:, :, 1], part_max[:], AX.X, ALU.max).then_inc(stats_ready, 1)
                dve.wait_ge(summed, 1 + 10 * b + 10)
                dve.tensor_reduce(stats[:, :, 0], part_sum[:], AX.X, ALU.add).then_inc(stat_steps, 1)
                dve.wait_ge(stat_steps, b + 1)
                dve.tensor_scalar(stats[:, :, 0], stats[:, :, 0], 1.0 / PXS, None, ALU.mult).then_inc(stats_ready, 1)
                dve.wait_ge(mlp1_done, b + 1)
                dve.tensor_scalar(hidden[:], BANK[5][0:HID, 0:2], 0.0, None, ALU.max).then_inc(gate_steps, 1)
                dve.wait_ge(gate_steps, 3 * b + 1)
                dve.tensor_tensor(hidden_sum[:], hidden[:, 0:1], hidden[:, 1:2], ALU.add).then_inc(mlp1_ready, 1)
                dve.wait_ge(gate_exp, b + 1)
                dve.tensor_scalar(chan_gate[:], chan_gate[:], 1.0, None, ALU.add).then_inc(gate_steps, 1)
                dve.wait_ge(gate_steps, 3 * b + 2)
                dve.reciprocal(chan_gate[:], chan_gate[:]).then_inc(gate_steps, 1)
                dve.wait_ge(gate_steps, 3 * b + 3)
                for t in range(CT):
                    dve.tensor_scalar(p_hi[:, t, :], proj[:, t, :], chan_gate[:, t:t + 1], None, ALU.mult).then_inc(
                        proj_hi_ready, 1)
                for t in range(CT):
                    dve.wait_ge(proj_hi_ready, 2 * b + 1 + t)
                    dve.scalar_tensor_tensor(out=p_lo[:, t, :], in0=proj[:, t, :], scalar=chan_gate[:, t:t + 1],
                                             in1=p_hi[:, t, :].bitcast(F32), op0=ALU.mult,
                                             op1=ALU.subtract).then_inc(proj_ready, 1)

                def low_half(i, k):
                    dve.wait_ge(s_hi_ready, b * 20 + 2 * i + k + 1)
                    dve.tensor_tensor(s_lo[k][:], fused[:, :, bass.ds((2 * i + k) * PX, PX)],
                                      s_hi[k][:].bitcast(F32), ALU.subtract).then_inc(s_ready, 1)

                def butterfly(i, k):
                    s = b * 20 + 2 * i + k
                    for n in range(8):
                        dve.wait_ge(comp_used[n], 1 + s + 1)
                    dve.wait_ge(haar_ready, 1 + s)
                    for t in range(CT):
                        for n, op in enumerate((ALU.add, ALU.subtract)):
                            dve.tensor_tensor(pairs[:, t, 2 * n:2 * n + 2, :], comp[k][:, t, 0:3:2, :],
                                              comp[k][:, t, 1:4:2, :], op).then_inc(pairs_ready, 1)
                    for t in range(CT):
                        dve.wait_ge(pairs_ready, 4 * s + 2 * t + 2)
                        for n, op in enumerate((ALU.add, ALU.subtract)):
                            last = dve.tensor_tensor(comp[k][:, t, 2 * n:2 * n + 2, :], pairs[:, t, 0:3:2, :],
                                                     pairs[:, t, 1:4:2, :], op)
                    last.then_inc(haar_ready, 1)

                low_half(0, 0)
                with dve.Fori(0, LAST) as i:
                    for k in range(2):
                        low_half(*after(i, k, 1))
                        butterfly(i, k)
                low_half(LAST, 1)
                butterfly(LAST, 0)
                butterfly(LAST, 1)

        @block.gpsimd
        def _(pool):
            for semaphore in FROM_ONE:
                pool.sem_inc(semaphore, 1)
            with pool.Fori(0, B) as b:
                def pick(i, k):
                    pool.tensor_copy(key_max_now[k][:], key_max[:, bass.ds(2 * i + k, 1), :].rearrange(
                        "p s t -> p (s t)")).then_inc(keymax_now, 1)

                def keep(i, k):
                    s = b * 20 + 2 * i + k
                    wait_alone(pool, (conv_used[0], s * 5 + 1), (conv_used[1], s * 5 + 1))
                    pool.tensor_copy(fused[:, :, bass.ds((2 * i + k) * PX, PX)], fused_now[k][:]).then_inc(fused_kept, 1)

                wait_alone(pool, (keymax_ready, b * 20 + 20), (s_ready, b * 20))
                for k in range(2):
                    pick(0, k)
                with pool.Fori(0, LAST) as i:
                    for k in range(2):
                        wait_alone(pool, (spread_used, (b * 20 + 2 * i + k + 1) * 3))
                        pick(i + 1, k)
                        keep(i, k)
                for k in range(2):
                    keep(LAST, k)
                with pool.Fori(0, S // 2) as i:
                    for k in range(2):
                        pool.wait_ge(haar_ready, 1 + b * 20 + 2 * i + k + 1)
                        pool.wait_ge(ring_loaded[k], (b * 30 + 20 + i + 1) * 16)
                        pool.tensor_tensor(slot(k), slot(k), comp[k][:].rearrange("p t a n -> p (t a n)").rearrange(
                            "p (r c) -> p r c", c=C), ALU.add).then_inc(added[k], 1)

        @block.scalar
        def _(act):
            act.wait_ge(prep, VAR_READY[0])
            act.activation(small[:, 0:10], small[:, 0:10], ACT.Sqrt).then_inc(prep_root, 1)
            act.wait_ge(prep, PREP_DONE[0])
            with act.Fori(0, B) as b:
                with act.Fori(0, S // 2) as i:
                    for k in range(2):
                        act.wait_ge(shifted, b * 20 + 2 * i + k + 1)
                        act.activation(expo[k][:], expo[k][:], ACT.Exp).then_inc(expo_ready, 1)

                def exp_keys(i, k):
                    for n in range(3):
                        act.wait_ge(spread_used, 1 + (b * 20 + 2 * i + k) * 3 + n + 1)
                        piece = slot4(k)[:, :, 2 * n:2 * n + min(2, JC - 2 * n), :]
                        act.activation(piece, piece, ACT.Exp).then_inc(keys_ready, 1)

                def evacuate(i, k):
                    s = b * 20 + 2 * i + k
                    for t in range(CT):
                        act.wait_ge(conv_done[t], 1 + s * 5 + 1)
                        if not isinstance(i, int) or i:
                            act.wait_ge(fused_kept, 1 + s - 1)
                            act.wait_ge(px_done, 1 + 2 * s - 2)
                        act.activation(fused_now[k][:, t, :], conv_bank[t][:, 0:PX], ACT.Relu, bias=bias1[:, t:t + 1],
                                       scale=scale1[:, t:t + 1]).then_inc(conv_used[t], 1)
                    for t in range(CT):
                        act.wait_ge(y_stored[t], 1 + s * 16)
                        for q in range(4):
                            act.wait_ge(conv_done[q % 2], 1 + s * 5 + 2 + 2 * t + q // 2)
                            act.activation(y_out[t][:, q * PX:(q + 1) * PX], conv_bank[q % 2][:, 0:PX], ACT.Identity,
                                           bias=vec[:, VEC["conv_b"] + t:VEC["conv_b"] + t + 1]).then_inc(
                                               conv_used[q % 2], 1)

                exp_keys(0, 0)
                exp_keys(0, 1)
                act.wait_ge(fused_kept, 1 + 20 * b)
                act.wait_ge(px_done, 1 + 40 * b)
                for k in range(2):
                    exp_keys(1, k)
                    evacuate(0, k)
                with act.Fori(1, LAST) as i:
                    for k in range(2):
                        exp_keys(i + 1, k)
                        evacuate(i, k)
                for k in range(2):
                    evacuate(LAST, k)

                act.wait_ge(att_done, b + 1)
                act.activation(sig[:], BANK[4][0:H2, 0:W2], ACT.Exp, scale=-1.0).then_inc(att_exp, 1)
                n = PXS // JC
                for q in range(JC):
                    for t in range(CT):
                        act.wait_ge(gated, 10 * b + 2 * q + t + 1)
                        act.wait_ge(summed, 1 + 10 * b + 2 * q + t)
                        act.activation(junk[:], fused[:, t, q * n:(q + 1) * n], ACT.Copy,
                                       accum_out=part_sum[:, t, q:q + 1]).then_inc(summed, 1)
                act.wait_ge(mlp2_done, b + 1)
                act.activation(chan_gate[:], BANK[6][:, 0:CT], ACT.Exp, scale=-1.0).then_inc(gate_exp, 1)

                def high_half(i, k):
                    act.wait_ge(comp_done[7], 1 + (b * 20 if isinstance(i, int) and i == 0 else b * 20 + 2 * i + k - 1))
                    act.activation(s_hi[k][:], fused[:, :, bass.ds((2 * i + k) * PX, PX)], ACT.Copy).then_inc(
                        s_hi_ready, 1)

                def components(i, k):
                    s = b * 20 + 2 * i + k
                    act.wait_ge(added[k], 1 + b * 10 + i)
                    for n in range(8):
                        act.wait_ge(comp_done[n], 1 + s + 1)
                        act.activation(comp[k][:, n % 2, n // 2, :], BANK[n][:, 0:PX], ACT.Relu,
                                       bias=bias2[:, n:n + 1], scale=scale2[:, n:n + 1]).then_inc(comp_used[n], 1)

                high_half(0, 0)
                with act.Fori(0, LAST) as i:
                    for k in range(2):
                        high_half(*after(i, k, 1))
                        components(i, k)
                high_half(LAST, 1)
                components(LAST, 0)
                components(LAST, 1)

        @block.tensor
        def _(pe):
            pe.wait_ge(prep, FQ_READY[0])
            for n in range(4):
                t, q0 = n // 2, n % 2 * 2
                for q in range(2):
                    for m in range(CT):
                        last = pe.matmul(BANK[n][:, q * C:(q + 1) * C], wn[:, m, t * P:(t + 1) * P], fq[:, q0 + q, m, :],
                                         start=(m == 0), stop=(m == CT - 1))
                last.then_inc(prep_mm, 1)
            for t in range(CT):
                for q in range(4):
                    for m in range(CT):
                        last = pe.matmul(BANK[4 + t][:, 0:1], fq[:, q, m, t * P:(t + 1) * P],
                                         vec[:, VEC["conv_b"] + m:VEC["conv_b"] + m + 1],
                                         start=(q == 0 and m == 0), stop=(q == 3 and m == CT - 1))
                last.then_inc(prep_mm, 1)
            pe.wait_ge(prep, PREP_DONE[0])

            with pe.Fori(0, B) as b:
                for n in range(8):
                    pe.wait_ge(comp_used[n], 1 + 20 * b)
                pe.wait_ge(chan_max_ready, b + 1)
                for t in range(CT):
                    last = pe.transpose(max_bank[0][:, t * P:(t + 1) * P], chan_max[:, t:t + 1].broadcast_to([P, P]),
                                        ident[:])
                last.then_inc(m_row_done, 1)

                def accumulate(i, k, first=False, final=False):
                    pe.wait_ge(expo_ready, b * 20 + 2 * i + k + 1)
                    for r in range(TILES):
                        for t in range(CT):
                            last = pe.matmul(acc[t][:, 0:C + 1], expo[k][:, r, t * P:(t + 1) * P],
                                             load_ring[k][:, r, :], start=(first and r == 0),
                                             stop=(final and r == TILES - 1))
                    last.then_inc(rows_used[k], 1)

                accumulate(0, 0, first=True)
                accumulate(0, 1)
                with pe.Fori(1, LAST) as i:
                    for k in range(2):
                        accumulate(i, k)
                accumulate(LAST, 0)
                accumulate(LAST, 1, final=True)
                pe.wait_ge(vq_scaled, 2 * b + 2)
                for t in range(CT):
                    for d in range(CT):
                        last = pe.transpose(conv_bank[t][:, d * P:(d + 1) * P], vqT[:, d, t * P:(t + 1) * P], ident[:])
                last.then_inc(vq_turned, 1)

                def spread_maxima(i, k):
                    s = b * 20 + 2 * i + k
                    pe.wait_ge(keymax_now, 1 + s + 1)
                    pe.wait_ge(spread_used, 1 + s * 3)
                    for j in range(JC):
                        for h in range(CT):
                            n = (j % 2) * C + h * P
                            last = pe.transpose(max_bank[j // 2][:, n:n + P],
                                                key_max_now[k][:, h * JC + j:h * JC + j + 1].broadcast_to([P, P]), ident[:])
                        if j % 2 or j == JC - 1:
                            last.then_inc(spread, 1)

                def attend(i, k):
                    s = b * 20 + 2 * i + k
                    pe.wait_ge(keys_ready, s * 3 + 3)
                    for j in range(JC):
                        for h in range(CT):
                            pe.wait_ge(attn_used[h], 1 + s * JC + j)
                            for t in range(CT):
                                last = pe.matmul(acc[h][:, 0:C + 1], load_ring[k][:, t * JC + j, h * P:(h + 1) * P],
                                                 vq[:, t, :], start=(t == 0), stop=(t == CT - 1))
                            last.then_inc(attn_done[h], 1)

                def product(dst, pairs_, done):
                    n = 0
                    for (a_hi, a_lo), (x_hi, x_lo) in pairs_:
                        for a, x in ((a_hi, x_hi), (a_hi, x_lo), (a_lo, x_hi)):
                            last = pe.matmul(dst, a, x, start=(n == 0), stop=(n == 3 * len(pairs_) - 1))
                            n += 1
                    last.then_inc(done, 1)

                def fuse(i, k):
                    s = b * 20 + 2 * i + k
                    pe.wait_ge(split_ready, 1 + s + 1)
                    for m in range(CT):
                        pe.wait_ge(conv_used[m], 1 + s * 5)
                        cols = slice(m * P, (m + 1) * P)
                        product(conv_bank[m][:, 0:PX],
                                [((g_hi[:, t, q, cols], g_lo[:, t, q, cols]),
                                  (parity(o_hi[k], t, q), parity(o_lo[k], t, q))) for q in range(4) for t in range(CT)],
                                conv_done[m])

                def convolve(i, k, m):
                    s = b * 20 + 2 * i + k
                    cols = slice(m * P, (m + 1) * P)
                    for n in range(4):
                        q = n % 2 * 2 + n // 2
                        pe.wait_ge(conv_used[n % 2], 1 + s * 5 + 1 + 2 * m + n // 2)
                        product(conv_bank[n % 2][:, 0:PX],
                                [((w_hi[:, t, cols], w_lo[:, t, cols]),
                                  (parity(o_hi[k], t, q), parity(o_lo[k], t, q))) for t in range(CT)],
                                conv_done[n % 2])

                def turn(i, k, n):
                    s = b * 20 + 2 * i + k
                    for t in range(CT):
                        pe.wait_ge(conv_used[t], 1 + s * 5 + 1)
                    pe.wait_ge(px_used, 1 + 2 * s + n)
                    for r in range(2):
                        for t in range(CT):
                            px = (2 * n + r) * W2
                            last = pe.transpose(px_bank[0:W2, r * C + t * P:r * C + (t + 1) * P],
                                                fused_now[k][:, t, px:px + W2], ident[:])
                    last.then_inc(px_done, 1)

                def conv_stage(i, k):
                    fuse(i, k)
                    convolve(i, k, 0)
                    turn(i, k, 0)
                    convolve(i, k, 1)
                    turn(i, k, 1)

                pe.wait_ge(m_row_ready, b + 1)
                spread_maxima(0, 0)
                spread_maxima(0, 1)
                pe.wait_ge(vq_ready, 2 * b + 2)
                attend(0, 0)
                with pe.Fori(0, LAST) as i:
                    for k in range(2):
                        spread_maxima(i + 1, k)
                        attend(*after(i, k, 1))
                        conv_stage(i, k)
                attend(LAST, 1)
                conv_stage(LAST, 0)
                conv_stage(LAST, 1)

                pe.wait_ge(maps_ready, b + 1)
                for m in range(2):
                    for ky in range(KS):
                        last = pe.matmul(BANK[4][0:H2, 0:W2], maps[:, m, ky:ky + H2], band[:, m * KS + ky, :],
                                         start=(m == 0 and ky == 0), stop=(m == 1 and ky == KS - 1))
                last.then_inc(att_done, 1)
                pe.wait_ge(stats_ready, 2 * b + 2)
                for t in range(CT):
                    last = pe.matmul(BANK[5][0:HID, 0:2], w1[:, t, :], stats[:, t, :], start=(t == 0), stop=(t == CT - 1))
                last.then_inc(mlp1_done, 1)
                pe.wait_ge(mlp1_ready, b + 1)
                for t in range(CT):
                    last = pe.matmul(BANK[6][:, t:t + 1], w2[:, t * P:(t + 1) * P], hidden_sum[:], start=True, stop=True)
                last.then_inc(mlp2_done, 1)

                wait_alone(pe, (gate_exp, b + 1), (proj_ready, 2 * b + 2))
                wait_alone(pe, (conv_used[0], 100 * b + 100), (conv_used[1], 100 * b + 100))
                with pe.Fori(0, S // 2) as i:
                    for k in range(2):
                        s = b * 20 + 2 * i + k
                        pe.wait_ge(s_ready, 1 + s + 1)
                        for n in range(8):
                            pe.wait_ge(comp_used[n], 1 + s)
                            cols = slice(n * P, (n + 1) * P)
                            for m, (a, x) in enumerate((a, x) for t in range(CT) for a, x in (
                                    (p_hi[:, t, cols], s_hi[k][:, t, :]), (p_hi[:, t, cols], s_lo[k][:, t, :]),
                                    (p_lo[:, t, cols], s_hi[k][:, t, :]))):
                                last = pe.matmul(BANK[n][:, 0:PX], a, x, start=(m == 0), stop=(m == 5))
                            last.then_inc(comp_done[n], 1)


def kernel(x, L0_conv_conv_w, L0_conv_conv_b, L0_conv_gamma, L1_conv_fusion_w, L1_conv_fusion_b, L1_conv_bn1_g,
           L1_conv_bn1_b, L1_conv_bn1_m, L1_conv_bn1_v, L1_conv_sa_w, L1_conv_ca_w1, L1_conv_ca_w2, L1_conv_proj_w,
           L1_conv_proj_b, L1_conv_bn2_g, L1_conv_bn2_b, L1_conv_bn2_m, L1_conv_bn2_v):
    import concourse.bacc as bacc
    from concourse.bass_utils import run_bass_kernel_spmd

    x = np.asarray(x)
    B = x.shape[0]
    blocks = x.reshape(B, CT, P, CT, P, S, JC)
    x_rows = blocks.transpose(0, 5, 4, 3, 6, 1, 2).reshape(B, S, P, CT * POS)
    x_keys = blocks.transpose(0, 5, 2, 1, 6, 3, 4).reshape(B, S, P, CT * POS)
    x_pos = np.zeros((B + 1, S, P, CT * POS), x.dtype)
    x_pos[:B] = x.reshape(B, CT, P, S, ROWS, W2, 2).transpose(0, 3, 2, 1, 6, 4, 5).reshape(B, S, P, CT * POS)

    def columns(v):
        return np.asarray(v).reshape(-1, P).T

    vectors = np.concatenate([columns(v) for v in (
        L0_conv_conv_b, L1_conv_fusion_b, L1_conv_bn1_g, L1_conv_bn1_b, L1_conv_bn1_m, L1_conv_bn1_v, L1_conv_proj_b,
        L1_conv_bn2_g, L1_conv_bn2_b, L1_conv_bn2_m, L1_conv_bn2_v)], axis=1)
    sa = np.asarray(L1_conv_sa_w)[0]
    bands = np.zeros((W2, 2 * KS, W2), sa.dtype)
    for m in range(2):
        for ky in range(KS):
            for w_out in range(W2):
                for kx in range(KS):
                    w_in = w_out + kx - PAD
                    if 0 <= w_in < W2:
                        bands[w_in, m * KS + ky, w_out] = sa[m, ky, kx]

    arrays = {
        "x_rows": x_rows, "x_keys": x_keys, "x_pos": x_pos, "conv_w": np.asarray(L0_conv_conv_w),
        "conv_wT": np.asarray(L0_conv_conv_w).T, "fusion_wT": np.asarray(L1_conv_fusion_w).T,
        "proj_wT": np.asarray(L1_conv_proj_w).T, "w1T": np.asarray(L1_conv_ca_w1).T,
        "w2T": np.asarray(L1_conv_ca_w2).T, "vectors": vectors, "gamma": np.asarray(L0_conv_gamma), "bands": bands,
        "identity": np.eye(P, dtype=np.float32),
    }
    arrays = {f"in_{k}": np.ascontiguousarray(v) for k, v in arrays.items()}
    nc = bacc.Bacc("TRN2", target_bir_lowering=False, num_devices=1)
    args = [nc.dram_tensor(k, v.shape, mybir.dt.from_np(v.dtype), kind="ExternalInput").ap() for k, v in arrays.items()]
    out = nc.dram_tensor("out", (B, S, P, CT * POS), F32, kind="ExternalOutput").ap()
    build(nc, B, *args, out)
    got = run_bass_kernel_spmd(nc, [arrays], core_ids=[0]).results[0]["out"]
    return np.ascontiguousarray(got.reshape(B, S, P, CT, 2, 2, HR, W2).transpose(0, 3, 2, 1, 6, 5, 7, 4)).reshape(B, C, H, W)
```

```python
from contextlib import ExitStack

import numpy as np

import concourse.bass as bass
from concourse import mybir

F32 = mybir.dt.float32
F32R = mybir.dt.float32r
ACT = mybir.ActivationFunctionType
ALU = mybir.AluOpType
AX = mybir.AxisListType

P = 128
C = 256
CT = C // P
H = W = 160
N = H * W
J = N // C
JC = 5
S = J // JC
POS = JC * C
ROWS = POS // W
W2 = W // 2
H2 = H // 2
HR = ROWS // 2
PX = HR * W2
HALF = POS // 2
PXS = H2 * W2
HID = C // 16
KS = 7
PAD = KS // 2
EPS = 1e-5
TILES = JC * CT
SLOTS = 4
LOADS = S // SLOTS + 2 * (S // 2)
LOWEST = -3.0e38
VEC = {"conv_b": 0, "fusion_b": 2, "bn1_g": 4, "bn1_b": 6, "bn1_m": 8, "bn1_v": 10,
       "proj_b": 12, "bn2_g": 20, "bn2_b": 28, "bn2_m": 36, "bn2_v": 44}
NVEC = 52


def build(nc, B, x_rows, x_keys, x_pos, conv_w, conv_wT, fusion_wT, proj_wT, w1T, w2T, vectors, gamma, bands,
          identity, out):
    y_dram = nc.dram_tensor("y_scratch", [B, S, P, CT * POS], F32).ap()
    sig_dram = nc.dram_tensor("sig_scratch", [B, H2, W2], F32).ap()

    FQ_READY, VAR_READY, PREP_DONE = [0], [0], [0]

    with ExitStack() as ctx:
        def sb(name, shape, dt=F32, stack=ctx):
            return stack.enter_context(nc.sbuf_tensor(name, shape, dt))

        def sem(name):
            return ctx.enter_context(nc.semaphore(name))

        def sems(name, n):
            return [sem(f"{name}{i}") for i in range(n)]

        ident = sb("ident", [P, P])
        vec = sb("vec", [P, NVEC])
        gam = sb("gam", [P, 1])
        w_hi = sb("w_hi", [P, CT, C], F32R)
        w_lo = sb("w_lo", [P, CT, C], F32R)
        g_hi = sb("g_hi", [P, CT, 4, C], F32R)
        g_lo = sb("g_lo", [P, CT, 4, C], F32R)
        proj = sb("proj", [P, CT, 4 * C])
        w1 = sb("w1", [P, CT, HID])
        w2 = sb("w2", [HID, C])
        band = sb("band", [W2, 2 * KS, W2])
        scale1 = sb("scale1", [P, CT])
        bias1 = sb("bias1", [P, CT])
        scale2 = sb("scale2", [P, 8])
        bias2 = sb("bias2", [P, 8])
        small = sb("small", [P, 16])

        load_ring = [sb(f"load_ring{k}", [P, TILES, C + 1]) for k in range(2)]
        fused = sb("fused", [P, CT, PXS])
        tile_max = sb("tile_max", [P, C])
        chunk_max = sb("chunk_max", [P, CT])
        chan_max = sb("chan_max", [P, SLOTS, CT])
        rescale = sb("rescale", [P, SLOTS, CT])
        m_row = [sb(f"m_row{k}", [P, C]) for k in range(2)]
        key_max = sb("key_max", [P, S, TILES])
        key_max_now = [sb(f"key_max_now{k}", [P, TILES]) for k in range(2)]
        vq_sum = sb("vq_sum", [P, CT])
        vq_scale = sb("vq_scale", [P, CT])
        vqT = sb("vqT", [P, CT, C + 1])
        vq = sb("vq", [P, CT, C + 1])
        attn_inv = sb("attn_inv", [P, CT])
        maps = sb("maps", [W2, 2, H2 + 2 * PAD])
        sig = sb("sig", [H2, W2])
        part_max = sb("part_max", [P, CT, JC])
        part_sum = sb("part_sum", [P, CT, JC])
        stats = sb("stats", [P, CT, 2])
        hidden = sb("hidden", [HID, 2])
        hidden_sum = sb("hidden_sum", [HID, 1])
        chan_gate = sb("chan_gate", [P, CT])

        with ExitStack() as area:
            more_rows = [sb(f"more_rows{k}", [P, TILES, C + 1], F32, area) for k in range(2)]
            with ExitStack() as sub:
                expo = [sb(f"expo{k}", [P, TILES, C], F32, sub) for k in range(2)]
            with ExitStack() as sub:
                fT = sb("fT", [P, 4, CT, C], F32, sub)
                fq = sb("fq", [P, 4, CT, C], F32, sub)
                ftmp = sb("ftmp", [P, 4, CT, C], F32, sub)
                wn = sb("wn", [P, CT, C], F32, sub)
                wt = sb("wt", [P, CT, C], F32, sub)
        with ExitStack() as area:
            out2 = [sb(f"out2_{k}", [P, CT, POS], F32, area) for k in range(2)]
            o_hi = [sb(f"o_hi{k}", [P, CT, POS], F32R, area) for k in range(2)]
            o_lo = [sb(f"o_lo{k}", [P, CT, POS], F32R, area) for k in range(2)]
            y_out = [sb(f"y_out{k}", [P, POS], F32, area) for k in range(CT)]
            fused_now = [sb(f"fused_now{k}", [P, CT, PX], F32, area) for k in range(2)]
        with ExitStack() as area:
            s_hi = [sb(f"s_hi{k}", [P, CT, PX], F32R, area) for k in range(2)]
            s_lo = [sb(f"s_lo{k}", [P, CT, PX], F32R, area) for k in range(2)]
            p_hi = sb("p_hi", [P, CT, 4 * C], F32R, area)
            p_lo = sb("p_lo", [P, CT, 4 * C], F32R, area)
            with ExitStack() as sub:
                sig_all = sb("sig_all", [P, PXS], F32, sub)
                junk = sb("junk", [P, 4 * PX], F32, sub)
            with ExitStack() as sub:
                comp = [sb(f"comp{k}", [P, CT, 4, PX], F32, sub) for k in range(2)]
                pairs = sb("pairs", [P, CT, 4, PX], F32, sub)
                result = [sb(f"result{k}", [P, CT, 4, PX], F32, sub) for k in range(2)]

        BANK = [ctx.enter_context(nc.psum_tensor(f"bank{i}", [P, 512], F32)) for i in range(8)]
        chunk_bank = (BANK[0:2], BANK[2:4])
        turned_bank = BANK[4]
        m_bank = BANK[5]
        acc = BANK[0:2]
        conv_bank = BANK[2:4]
        max_bank = BANK[4:7]
        px_bank = BANK[7]

        weights_loaded = sem("weights_loaded")
        ring_loaded = sems("ring_loaded", 2)
        more_loaded = sems("more_loaded", 2)
        pos_loaded = sems("pos_loaded", 2)
        sig_loaded = sems("sig_loaded", JC)
        y_stored = sems("y_stored", 2)
        out_stored = sems("out_stored", 2)
        sig_stored = sem("sig_stored")
        prep = sem("prep")
        prep_mm = sem("prep_mm")
        passed = sem("passed")
        prep_root = sem("prep_root")
        area_reset = sem("area_reset")
        reset = sem("reset")
        tile_max_ready = sem("tile_max_ready")
        turned = sem("turned")
        max_steps = sem("max_steps")
        chan_max_ready = sem("chan_max_ready")
        m_row_done = sem("m_row_done")
        m_row_ready = sem("m_row_ready")
        rescale_ready = sem("rescale_ready")
        keymax_ready = sem("keymax_ready")
        shifted = sems("shifted", 2)
        expo_ready = sem("expo_ready")
        product_done = sems("product_done", 2)
        merged = sems("merged", 2)
        vq_steps = sem("vq_steps")
        vq_scaled = sem("vq_scaled")
        vq_turned = sem("vq_turned")
        vq_ready = sem("vq_ready")
        keymax_now = sem("keymax_now")
        spread = sem("spread")
        spread_used = sem("spread_used")
        keys_ready = sem("keys_ready")
        attn_done = sems("attn_done", 2)
        attn_used = sems("attn_used", 2)
        inv_ready = sem("inv_ready")
        hi_ready = sem("hi_ready")
        split_ready = sem("split_ready")
        conv_done = sems("conv_done", 2)
        conv_used = sems("conv_used", 2)
        fused_kept = sem("fused_kept")
        px_done = sem("px_done")
        px_used = sem("px_used")
        maps_ready = sem("maps_ready")
        att_done = sem("att_done")
        att_exp = sem("att_exp")
        att_steps = sem("att_steps")
        sig_ready = sem("sig_ready")
        gated = sem("gated")
        summed = sem("summed")
        stat_steps = sem("stat_steps")
        stats_ready = sem("stats_ready")
        mlp1_done = sem("mlp1_done")
        mlp1_ready = sem("mlp1_ready")
        mlp2_done = sem("mlp2_done")
        gate_exp = sem("gate_exp")
        gate_steps = sem("gate_steps")
        proj_hi_ready = sem("proj_hi_ready")
        proj_ready = sem("proj_ready")
        s_hi_ready = sem("s_hi_ready")
        s_ready = sem("s_ready")
        comp_done = sems("comp_done", 8)
        comp_used = sems("comp_used", 8)
        pairs_ready = sem("pairs_ready")
        haar_done = sems("haar_done", 2)
        added = sems("added", 2)

        block = ctx.enter_context(nc.Block())

        def slot(k):
            return load_ring[k][:, :, 0:C]

        def slot4(k):
            return slot(k).rearrange("p (t r) c -> p t r c", t=CT)

        def block_of(tile, t, j):
            return tile[:, t, :].rearrange("p (w n) -> p w n", w=2)[:, :, j * P:(j + 1) * P]

        def parity(tile, t, q):
            half = tile[:, t, q % 2 * HALF:(q % 2 + 1) * HALF]
            return half.rearrange("p (h a w) -> p h a w", a=2, w=W2)[:, :, q // 2, :]

        def at(v, b, s):
            return v[bass.ds(b, 1), bass.ds(s, 1)].rearrange("b s p n -> p (b s n)")

        def at_t(v, b, t, s):
            return at(v, b, s)[:, t * POS:(t + 1) * POS]

        def after(i, k, n):
            return i + (k + n) // 2, (k + n) % 2

        LAST = S // 2 - 1

        rows = load_ring + more_rows
        rows_loaded = ring_loaded + more_loaded
        GROUPS = S // SLOTS

        def x_rows_of(k):
            return rows[k][:, :, 0:C]

        def before(i, k):
            return 2 * i + k // 2

        def rows_in(b, i, k):
            return (b * (LOADS if k < 2 else GROUPS) + i + 1) * 16

        def after4(i, k, n):
            return i + (k + n) // SLOTS, (k + n) % SLOTS

        def over_chunks(eng, step, last):
            with eng.Fori(0, last // SLOTS) as i:
                for k in range(SLOTS):
                    step(i, k)
            for k in range(last % SLOTS):
                step(last // SLOTS, k)

        def wait_alone(eng, *waits):
            for semaphore, value in waits:
                eng.wait_ge(semaphore, value + (1 if semaphore in FROM_ONE else 0))
                eng.sem_inc(passed, 1)

        FROM_ONE = [keymax_now, split_ready, px_done, px_used, fused_kept, spread_used, summed, s_ready, m_row_ready]
        for group in (shifted, product_done, merged, haar_done, attn_done, attn_used, conv_done, conv_used, comp_done,
                      comp_used, added, y_stored, out_stored):
            FROM_ONE += group

        @block.sync
        def _(sp):
            tiled = "(t p) o -> p t o"
            for dst, src in ((ident[:], identity), (vec[:], vectors),
                             (gam[:], gamma.rearrange("(a n) -> a n", a=1).broadcast_to([P, 1])),
                             (fT[:], fusion_wT.rearrange("(q t p) o -> p q t o", q=4, p=P)),
                             (wn[:], conv_w.rearrange(tiled, p=P)), (wt[:], conv_wT.rearrange(tiled, p=P)),
                             (proj[:], proj_wT.rearrange(tiled, p=P)), (w1[:], w1T.rearrange(tiled, p=P)),
                             (w2[:], w2T), (band[:], bands)):
                sp.dma_start(dst, src).then_inc(weights_loaded, 16)

            sp.wait_ge(prep, 1)
            with sp.Fori(0, B) as b:
                def load_rows(i, k):
                    sp.dma_start(x_rows_of(k), at(x_rows, b, SLOTS * i + k)).then_inc(rows_loaded[k], 16)

                for k in range(2):
                    wait_alone(sp, (added[k], b * 10))
                    load_rows(0, k)
                wait_alone(sp, (out_stored[0], b * 160), (out_stored[1], b * 160))
                for k in range(2, SLOTS):
                    load_rows(0, k)
                with sp.Fori(1, GROUPS) as i:
                    for k in range(SLOTS):
                        wait_alone(sp, (product_done[k % 2], b * 10 + before(i, k) - 1),
                                   (keymax_ready, b * 20 + SLOTS * (i - 1) + k + 1))
                        load_rows(i, k)

                def chunks_before(i, k):
                    return b * 20 if isinstance(i, int) and i == 0 else b * 20 + 2 * i + k - 1

                def load_keys(i, k):
                    sp.wait_ge(attn_done[1], 1 + chunks_before(i, k) * JC)
                    sp.dma_start(slot(k), at(x_keys, b, 2 * i + k)).then_inc(ring_loaded[k], 16)

                def load_pos(i, k):
                    sp.wait_ge(split_ready, 1 + chunks_before(i, k))
                    sp.dma_start(out2[k][:].rearrange("p t n -> p (t n)"), at(x_pos, b, 2 * i + k)).then_inc(pos_loaded[k], 16)

                def store_y(i, k):
                    s = b * 20 + 2 * i + k
                    for t in range(CT):
                        wait_alone(sp, (conv_used[0], s * 5 + 3 + 2 * t), (conv_used[1], s * 5 + 3 + 2 * t))
                        sp.dma_start(at_t(y_dram, b, t, 2 * i + k), y_out[t][:]).then_inc(y_stored[t], 16)

                wait_alone(sp, (product_done[0], b * 10 + 9), (product_done[1], b * 10 + 9), (keymax_ready, b * 20 + 18))
                for k in range(2):
                    load_keys(0, k)
                wait_alone(sp, (product_done[0], b * 10 + 10), (product_done[1], b * 10 + 10),
                           (keymax_ready, b * 20 + 20))
                for k in range(2):
                    load_pos(0, k)
                with sp.Fori(0, LAST) as i:
                    for k in range(2):
                        load_keys(i + 1, k)
                        load_pos(i + 1, k)
                        store_y(i, k)
                store_y(LAST, 0)
                store_y(LAST, 1)
                wait_alone(sp, (y_stored[0], 320 * b + 320), (y_stored[1], 320 * b + 320))

                sp.wait_ge(sig_ready, b + 1)
                sp.dma_start(sig_dram[bass.ds(b, 1)].rearrange("b h w -> h (b w)"), sig[:]).then_inc(sig_stored, 16)
                sp.wait_ge(sig_stored, 16 * b + 16)
                n = PXS // JC
                for q in range(JC):
                    sp.dma_start(sig_all[:, q * n:(q + 1) * n], sig_dram[bass.ds(b, 1)].rearrange(
                        "b h w -> b (h w)")[:, q * n:(q + 1) * n].broadcast_to([P, n])).then_inc(sig_loaded[q], 16)

                def load_y(i, k):
                    sp.dma_start(slot(k), at(y_dram, b, 2 * i + k)).then_inc(ring_loaded[k], 16)

                def store_out(i, k):
                    sp.wait_ge(added[k], 1 + b * 10 + i + 1)
                    sp.dma_start(at(out, b, 2 * i + k), result[k][:].rearrange("p t a n -> p (t a n)")).then_inc(
                        out_stored[k], 16)

                for k in range(2):
                    sp.wait_ge(attn_done[1], 1 + (b * 20 + 20) * JC)
                    load_y(0, k)
                with sp.Fori(0, LAST) as i:
                    for k in range(2):
                        store_out(i, k)
                        load_y(i + 1, k)
                for k in range(2):
                    store_out(LAST, k)
            for k in range(2):
                sp.wait_ge(out_stored[k], 1 + 160 * B)

        @block.vector
        def _(dve):
            steps = [0]

            def step(ins):
                steps[0] += 1
                ins.then_inc(prep, 1)
                dve.wait_ge(prep, steps[0])

            def col(name, n=CT):
                return vec[:, VEC[name]:VEC[name] + n]

            dve.memset(vq[:, :, C:C + 1], 1.0)
            dve.memset(load_ring[0][:, :, C:C + 1], 1.0)
            dve.memset(load_ring[1][:, :, C:C + 1], 1.0)
            step(dve.memset(maps[:], 0.0))
            dve.wait_ge(weights_loaded, 160)
            step(dve.tensor_tensor(ftmp[:, 0:2], fT[:, 0:3:2], fT[:, 1:4:2], ALU.add))
            step(dve.tensor_tensor(ftmp[:, 2:4], fT[:, 0:3:2], fT[:, 1:4:2], ALU.subtract))
            for n in range(2):
                step(dve.tensor_tensor(fq[:, 2 * n], ftmp[:, 2 * n], ftmp[:, 2 * n + 1], ALU.add))
                step(dve.tensor_tensor(fq[:, 2 * n + 1], ftmp[:, 2 * n], ftmp[:, 2 * n + 1], ALU.subtract))
            FQ_READY[0] = steps[0]
            step(dve.tensor_scalar(small[:, 0:2], col("bn1_v"), EPS, None, ALU.add))
            step(dve.tensor_scalar(small[:, 2:10], col("bn2_v", 8), EPS, None, ALU.add))
            VAR_READY[0] = steps[0]
            step(dve.tensor_copy(w_hi[:], wt[:]))
            step(dve.tensor_tensor(w_lo[:], wt[:], w_hi[:].bitcast(F32), ALU.subtract))
            dve.wait_ge(prep_root, 1)
            step(dve.reciprocal(small[:, 0:10], small[:, 0:10]))
            step(dve.tensor_tensor(scale1[:], small[:, 0:2], col("bn1_g"), ALU.mult))
            step(dve.tensor_tensor(scale2[:], small[:, 2:10], col("bn2_g", 8), ALU.mult))
            for n in range(4):
                t, q = n // 2, n % 2 * 2
                dve.wait_ge(prep_mm, n + 1)
                src = BANK[n][:].rearrange("p (q o) -> p q o", q=2)
                step(dve.tensor_copy(g_hi[:, t, q:q + 2, :], src))
                step(dve.tensor_tensor(g_lo[:, t, q:q + 2, :], src, g_hi[:, t, q:q + 2, :].bitcast(F32), ALU.subtract))
            dve.wait_ge(prep_mm, 6)
            for t in range(CT):
                step(dve.tensor_scalar(small[:, 10 + t:11 + t], BANK[4 + t][:, 0:1], 0.5, None, ALU.mult))
            step(dve.tensor_tensor(bias1[:], small[:, 10:12], col("fusion_b"), ALU.add))
            step(dve.tensor_tensor(bias1[:], bias1[:], col("bn1_m"), ALU.subtract))
            step(dve.tensor_tensor(bias1[:], bias1[:], scale1[:], ALU.mult))
            step(dve.tensor_tensor(bias1[:], bias1[:], col("bn1_b"), ALU.add))
            step(dve.tensor_scalar(scale1[:], scale1[:], 0.5, None, ALU.mult))
            step(dve.tensor_tensor(bias2[:], col("proj_b", 8), col("bn2_m", 8), ALU.subtract))
            step(dve.tensor_tensor(bias2[:], bias2[:], scale2[:], ALU.mult))
            step(dve.tensor_tensor(bias2[:], bias2[:], col("bn2_b", 8), ALU.add))
            step(dve.tensor_scalar(bias2[:], bias2[:], 0.5, None, ALU.mult))
            step(dve.tensor_scalar(scale2[:], scale2[:], 0.5, None, ALU.mult))
            PREP_DONE[0] = steps[0]

            with dve.Fori(0, B) as b:
                dve.memset(chan_max[:, SLOTS - 1, :], LOWEST).then_inc(reset, 1)
                dve.memset(vqT[:], 0.0).then_inc(reset, 1)
                dve.wait_ge(reset, 2 * b + 2)
                wait_alone(dve, (keymax_now, 20 * b))

                def maxima(i, k):
                    s = b * 20 + SLOTS * i + k
                    dve.wait_ge(rows_loaded[k], rows_in(b, i, k))
                    dve.tensor_reduce(tile_max[:], x_rows_of(k).rearrange("p r c -> p c r"), AX.X, ALU.max).then_inc(
                        tile_max_ready, 1)
                    dve.wait_ge(turned, s + 1)
                    dve.tensor_reduce(chunk_max[:], turned_bank[:, 0:C].rearrange("p (t n) -> p t n", t=CT), AX.X,
                                      ALU.max).then_inc(max_steps, 1)
                    dve.wait_ge(max_steps, 2 * s + 1)
                    m_before = chan_max[:, (k - 1) % SLOTS, :]
                    dve.tensor_tensor(chan_max[:, k, :], m_before, chunk_max[:], ALU.max).then_inc(chan_max_ready, 1)
                    dve.wait_ge(chan_max_ready, s + 1)
                    dve.tensor_tensor(rescale[:, k, :], m_before, chan_max[:, k, :], ALU.subtract).then_inc(max_steps, 1)
                    dve.tensor_reduce(key_max[:, bass.ds(SLOTS * i + k, 1), :].rearrange("p s t -> p (s t)"),
                                      x_rows_of(k), AX.X, ALU.max).then_inc(keymax_ready, 1)

                def merge(i, k):
                    s = b * 20 + SLOTS * i + k
                    dve.wait_ge(rescale_ready, s + 1)
                    dve.wait_ge(product_done[k % 2], 1 + b * 10 + before(i, k) + 1)
                    dve.wait_ge(merged[(k + 1) % 2], 1 + CT * (b * 10 + 2 * i + (k + 1) // 2))
                    for t in range(CT):
                        dve.scalar_tensor_tensor(out=vqT[:, t, :], in0=vqT[:, t, :], scalar=rescale[:, k, t:t + 1],
                                                 in1=chunk_bank[k % 2][t][:, 0:C + 1], op0=ALU.mult,
                                                 op1=ALU.add).then_inc(merged[k % 2], 1)

                maxima(0, 0)
                maxima(0, 1)

                def both(i, k):
                    maxima(*after4(i, k, 2))
                    merge(i, k)

                over_chunks(dve, both, S - 2)
                merge(GROUPS - 1, SLOTS - 2)
                merge(GROUPS - 1, SLOTS - 1)

                for k in range(2):
                    dve.wait_ge(merged[k], 1 + CT * (b * 10 + 10))
                dve.reciprocal(vq_sum[:], vqT[:, :, C]).then_inc(vq_steps, 1)
                dve.wait_ge(vq_steps, 2 * b + 1)
                dve.tensor_scalar(vq_scale[:], vq_sum[:], gam[:, 0:1], None, ALU.mult).then_inc(vq_steps, 1)
                dve.wait_ge(vq_steps, 2 * b + 2)
                for t in range(CT):
                    dve.tensor_scalar(vqT[:, t, 0:C], vqT[:, t, 0:C], vq_scale[:, t:t + 1], None, ALU.mult).then_inc(
                        vq_scaled, 1)

                def shift_keys(i, k):
                    s = b * 20 + 2 * i + k
                    dve.wait_ge(ring_loaded[k], (b * LOADS + GROUPS + i + 1) * 16)
                    for n in range(3):
                        dve.wait_ge(spread, s * 3 + n + 1)
                        r = min(2, JC - 2 * n)
                        piece = slot4(k)[:, :, 2 * n:2 * n + r, :]
                        dve.tensor_tensor(piece, piece, max_bank[n][:, 0:r * C].rearrange(
                            "p (a r c) -> p a r c", a=1, c=C).broadcast_to([P, CT, r, C]),
                            ALU.subtract).then_inc(spread_used, 1)

                def add_attention(i, k):
                    s = b * 20 + 2 * i + k
                    dve.wait_ge(pos_loaded[k], (b * 10 + i + 1) * 16)
                    for j in range(JC):
                        for t in range(CT):
                            dve.wait_ge(attn_done[t], 1 + s * JC + j + 1)
                            dve.reciprocal(attn_inv[:, t:t + 1], acc[t][:, C:C + 1]).then_inc(inv_ready, 1)
                            dve.wait_ge(inv_ready, (s * JC + j) * CT + t + 1)
                            o = block_of(out2[k], t, j)
                            dve.scalar_tensor_tensor(out=o, in0=acc[t][:, 0:C].rearrange("p (w n) -> p w n", w=2),
                                                     scalar=attn_inv[:, t:t + 1], in1=o, op0=ALU.mult,
                                                     op1=ALU.add).then_inc(attn_used[t], 1)

                def split(i, k):
                    s = b * 20 + 2 * i + k
                    for t in range(CT):
                        dve.wait_ge(attn_used[t], 1 + (s + 1) * JC)
                    dve.wait_ge(conv_done[1], 1 + ((b * 20 if isinstance(i, int) and i == 0 else s - 1) * 5))
                    dve.tensor_copy(o_hi[k][:], out2[k][:]).then_inc(hi_ready, 1)
                    dve.wait_ge(hi_ready, s + 1)
                    dve.tensor_tensor(o_lo[k][:], out2[k][:], o_hi[k][:].bitcast(F32), ALU.subtract).then_inc(
                        split_ready, 1)

                def map_rows(i, k, n):
                    s = b * 20 + 2 * i + k
                    dve.wait_ge(px_done, 1 + 2 * s + n + 1)
                    src = px_bank[0:W2, :].rearrange("p (r c) -> p r c", c=C)
                    at_row = (2 * i + k) * HR + 2 * n + PAD
                    dve.tensor_reduce(maps[:, 1, bass.ds(at_row, 2)], src, AX.X, ALU.max)
                    dve.tensor_reduce(maps[:, 0, bass.ds(at_row, 2)], src, AX.X, ALU.add).then_inc(px_used, 1)

                def rest(i, k):
                    map_rows(i, k, 0)
                    map_rows(i, k, 1)

                shift_keys(0, 0)
                dve.wait_ge(vq_turned, b + 1)
                for t in range(CT):
                    dve.tensor_copy(vq[:, t, 0:C].rearrange("p (w n) -> p w n", w=2),
                                    conv_bank[t][:, 0:C].rearrange("p (n w) -> p w n", w=2)).then_inc(vq_ready, 1)
                add_attention(0, 0)
                shift_keys(0, 1)
                split(0, 0)
                with dve.Fori(0, LAST) as i:
                    for k in range(2):
                        add_attention(*after(i, k, 1))
                        shift_keys(i + 1, k)
                        split(*after(i, k, 1))
                        rest(i, k)
                add_attention(LAST, 1)
                split(LAST, 1)
                rest(LAST, 0)
                rest(LAST, 1)

                dve.wait_ge(px_used, 1 + 40 * b + 40)
                dve.tensor_scalar(maps[:, 0, PAD:PAD + H2], maps[:, 0, PAD:PAD + H2], 1.0 / C, None, ALU.mult).then_inc(
                    maps_ready, 1)
                dve.wait_ge(att_exp, b + 1)
                dve.tensor_scalar(sig[:], sig[:], 1.0, None, ALU.add).then_inc(att_steps, 1)
                dve.wait_ge(att_steps, b + 1)
                dve.reciprocal(sig[:], sig[:]).then_inc(sig_ready, 1)
                wait_alone(dve, (fused_kept, 20 * b + 20))
                n = PXS // JC
                for q in range(JC):
                    wait_alone(dve, (sig_loaded[q], 16 * b + 16))
                    for t in range(CT):
                        f = fused[:, t, q * n:(q + 1) * n]
                        dve.tensor_tensor_reduce(f, f, sig_all[:, q * n:(q + 1) * n], 1.0, 0.0, ALU.mult, ALU.max,
                                                 part_max[:, t, q:q + 1]).then_inc(gated, 1)
                dve.wait_ge(gated, 10 * b + 10)
                dve.tensor_reduce(stats[:, :, 1], part_max[:], AX.X, ALU.max).then_inc(stats_ready, 1)
                dve.wait_ge(summed, 1 + 10 * b + 10)
                dve.tensor_reduce(stats[:, :, 0], part_sum[:], AX.X, ALU.add).then_inc(stat_steps, 1)
                dve.wait_ge(stat_steps, b + 1)
                dve.tensor_scalar(stats[:, :, 0], stats[:, :, 0], 1.0 / PXS, None, ALU.mult).then_inc(stats_ready, 1)
                dve.wait_ge(mlp1_done, b + 1)
                dve.tensor_scalar(hidden[:], BANK[5][0:HID, 0:2], 0.0, None, ALU.max).then_inc(gate_steps, 1)
                dve.wait_ge(gate_steps, 3 * b + 1)
                dve.tensor_tensor(hidden_sum[:], hidden[:, 0:1], hidden[:, 1:2], ALU.add).then_inc(mlp1_ready, 1)
                dve.wait_ge(gate_exp, b + 1)
                dve.tensor_scalar(chan_gate[:], chan_gate[:], 1.0, None, ALU.add).then_inc(gate_steps, 1)
                dve.wait_ge(gate_steps, 3 * b + 2)
                dve.reciprocal(chan_gate[:], chan_gate[:]).then_inc(gate_steps, 1)
                dve.wait_ge(gate_steps, 3 * b + 3)
                for t in range(CT):
                    dve.tensor_scalar(p_hi[:, t, :], proj[:, t, :], chan_gate[:, t:t + 1], None, ALU.mult).then_inc(
                        proj_hi_ready, 1)
                for t in range(CT):
                    dve.wait_ge(proj_hi_ready, 2 * b + 1 + t)
                    dve.scalar_tensor_tensor(out=p_lo[:, t, :], in0=proj[:, t, :], scalar=chan_gate[:, t:t + 1],
                                             in1=p_hi[:, t, :].bitcast(F32), op0=ALU.mult,
                                             op1=ALU.subtract).then_inc(proj_ready, 1)

                def low_half(i, k):
                    dve.wait_ge(s_hi_ready, b * 20 + 2 * i + k + 1)
                    dve.tensor_tensor(s_lo[k][:], fused[:, :, bass.ds((2 * i + k) * PX, PX)],
                                      s_hi[k][:].bitcast(F32), ALU.subtract).then_inc(s_ready, 1)

                def butterfly(i, k):
                    s = b * 20 + 2 * i + k
                    for n in range(8):
                        dve.wait_ge(comp_used[n], 1 + s + 1)
                    dve.wait_ge(haar_done[1 - k], 1 + b * 10 + i + k)
                    for t in range(CT):
                        for n, op in enumerate((ALU.add, ALU.subtract)):
                            dve.tensor_tensor(pairs[:, t, 2 * n:2 * n + 2, :], comp[k][:, t, 0:3:2, :],
                                              comp[k][:, t, 1:4:2, :], op).then_inc(pairs_ready, 1)
                    dve.wait_ge(out_stored[k], 1 + (b * 10 + i) * 16)
                    for t in range(CT):
                        dve.wait_ge(pairs_ready, 4 * s + 2 * t + 2)
                        for n, op in enumerate((ALU.add, ALU.subtract)):
                            last = dve.tensor_tensor(result[k][:, t, 2 * n:2 * n + 2, :], pairs[:, t, 0:3:2, :],
                                                     pairs[:, t, 1:4:2, :], op)
                    last.then_inc(haar_done[k], 1)

                low_half(0, 0)
                with dve.Fori(0, LAST) as i:
                    for k in range(2):
                        low_half(*after(i, k, 1))
                        butterfly(i, k)
                low_half(LAST, 1)
                butterfly(LAST, 0)
                butterfly(LAST, 1)

        @block.gpsimd
        def _(pool):
            for semaphore in FROM_ONE:
                pool.sem_inc(semaphore, 1)
            pool.wait_ge(prep, PREP_DONE[0])
            with pool.Fori(0, B) as b:
                wait_alone(pool, (out_stored[0], 160 * b), (out_stored[1], 160 * b))
                for k in range(2):
                    pool.memset(more_rows[k][:, :, C:C + 1], 1.0).then_inc(area_reset, 1)

                def shift_rows(i, k):
                    wait_alone(pool, (product_done[k % 2], b * 10 + before(i, k)),
                               (m_row_ready, b * 20 + SLOTS * i + k + 1))
                    pool.tensor_tensor(expo[k % 2][:], x_rows_of(k), m_row[k % 2][:].rearrange(
                        "p (a c) -> p a c", a=1).broadcast_to([P, TILES, C]), ALU.subtract).then_inc(shifted[k % 2], 1)

                over_chunks(pool, shift_rows, S)

                def pick(i, k):
                    pool.tensor_copy(key_max_now[k][:], key_max[:, bass.ds(2 * i + k, 1), :].rearrange(
                        "p s t -> p (s t)")).then_inc(keymax_now, 1)

                def keep(i, k):
                    s = b * 20 + 2 * i + k
                    wait_alone(pool, (conv_used[0], s * 5 + 1), (conv_used[1], s * 5 + 1))
                    pool.tensor_copy(fused[:, :, bass.ds((2 * i + k) * PX, PX)], fused_now[k][:]).then_inc(fused_kept, 1)

                wait_alone(pool, (keymax_ready, b * 20 + 20), (s_ready, b * 20))
                for k in range(2):
                    pick(0, k)
                with pool.Fori(0, LAST) as i:
                    for k in range(2):
                        wait_alone(pool, (spread_used, (b * 20 + 2 * i + k + 1) * 3))
                        pick(i + 1, k)
                        keep(i, k)
                for k in range(2):
                    keep(LAST, k)
                with pool.Fori(0, S // 2) as i:
                    for k in range(2):
                        pool.wait_ge(haar_done[k], 1 + b * 10 + i + 1)
                        pool.wait_ge(ring_loaded[k], (b * LOADS + GROUPS + S // 2 + i + 1) * 16)
                        r = result[k][:].rearrange("p t a n -> p (t a n)").rearrange("p (r c) -> p r c", c=C)
                        pool.tensor_tensor(r, slot(k), r, ALU.add).then_inc(added[k], 1)

        @block.scalar
        def _(act):
            act.wait_ge(prep, VAR_READY[0])
            act.activation(small[:, 0:10], small[:, 0:10], ACT.Sqrt).then_inc(prep_root, 1)
            act.wait_ge(prep, PREP_DONE[0])
            with act.Fori(0, B) as b:
                def scales(i, k):
                    s = b * 20 + SLOTS * i + k
                    act.wait_ge(m_row_done, s + 1)
                    act.wait_ge(shifted[k % 2], 1 + b * 10 + before(i, k))
                    act.activation(m_row[k % 2][:], m_bank[:, 0:C], ACT.Copy).then_inc(m_row_ready, 1)
                    act.wait_ge(max_steps, 2 * s + 2)
                    act.activation(rescale[:, k, :], rescale[:, k, :], ACT.Exp).then_inc(rescale_ready, 1)

                def exponentials(i, k):
                    act.wait_ge(shifted[k % 2], 1 + b * 10 + before(i, k) + 1)
                    act.activation(expo[k % 2][:], expo[k % 2][:], ACT.Exp).then_inc(expo_ready, 1)

                scales(0, 0)
                scales(0, 1)
                exponentials(0, 0)

                def both(i, k):
                    exponentials(*after4(i, k, 1))
                    scales(*after4(i, k, 2))

                over_chunks(act, both, S - 2)
                exponentials(GROUPS - 1, SLOTS - 1)

                def exp_keys(i, k):
                    for n in range(3):
                        act.wait_ge(spread_used, 1 + (b * 20 + 2 * i + k) * 3 + n + 1)
                        piece = slot4(k)[:, :, 2 * n:2 * n + min(2, JC - 2 * n), :]
                        act.activation(piece, piece, ACT.Exp).then_inc(keys_ready, 1)

                def evacuate(i, k):
                    s = b * 20 + 2 * i + k
                    for t in range(CT):
                        act.wait_ge(conv_done[t], 1 + s * 5 + 1)
                        if not isinstance(i, int) or i:
                            act.wait_ge(fused_kept, 1 + s - 1)
                            act.wait_ge(px_done, 1 + 2 * s - 2)
                        act.activation(fused_now[k][:, t, :], conv_bank[t][:, 0:PX], ACT.Relu, bias=bias1[:, t:t + 1],
                                       scale=scale1[:, t:t + 1]).then_inc(conv_used[t], 1)
                    for t in range(CT):
                        act.wait_ge(y_stored[t], 1 + s * 16)
                        for q in range(4):
                            act.wait_ge(conv_done[q % 2], 1 + s * 5 + 2 + 2 * t + q // 2)
                            act.activation(y_out[t][:, q * PX:(q + 1) * PX], conv_bank[q % 2][:, 0:PX], ACT.Identity,
                                           bias=vec[:, VEC["conv_b"] + t:VEC["conv_b"] + t + 1]).then_inc(
                                               conv_used[q % 2], 1)

                exp_keys(0, 0)
                exp_keys(0, 1)
                act.wait_ge(fused_kept, 1 + 20 * b)
                act.wait_ge(px_done, 1 + 40 * b)
                for k in range(2):
                    exp_keys(1, k)
                    evacuate(0, k)
                with act.Fori(1, LAST) as i:
                    for k in range(2):
                        exp_keys(i + 1, k)
                        evacuate(i, k)
                for k in range(2):
                    evacuate(LAST, k)

                act.wait_ge(att_done, b + 1)
                act.activation(sig[:], BANK[4][0:H2, 0:W2], ACT.Exp, scale=-1.0).then_inc(att_exp, 1)
                n = PXS // JC
                for q in range(JC):
                    for t in range(CT):
                        act.wait_ge(gated, 10 * b + 2 * q + t + 1)
                        act.wait_ge(summed, 1 + 10 * b + 2 * q + t)
                        act.activation(junk[:], fused[:, t, q * n:(q + 1) * n], ACT.Copy,
                                       accum_out=part_sum[:, t, q:q + 1]).then_inc(summed, 1)
                act.wait_ge(mlp2_done, b + 1)
                act.activation(chan_gate[:], BANK[6][:, 0:CT], ACT.Exp, scale=-1.0).then_inc(gate_exp, 1)

                def high_half(i, k):
                    act.wait_ge(comp_done[7], 1 + (b * 20 if isinstance(i, int) and i == 0 else b * 20 + 2 * i + k - 1))
                    act.activation(s_hi[k][:], fused[:, :, bass.ds((2 * i + k) * PX, PX)], ACT.Copy).then_inc(
                        s_hi_ready, 1)

                def components(i, k):
                    s = b * 20 + 2 * i + k
                    act.wait_ge(haar_done[k], 1 + b * 10 + i)
                    for n in range(8):
                        act.wait_ge(comp_done[n], 1 + s + 1)
                        act.activation(comp[k][:, n % 2, n // 2, :], BANK[n][:, 0:PX], ACT.Relu,
                                       bias=bias2[:, n:n + 1], scale=scale2[:, n:n + 1]).then_inc(comp_used[n], 1)

                high_half(0, 0)
                with act.Fori(0, LAST) as i:
                    for k in range(2):
                        high_half(*after(i, k, 1))
                        components(i, k)
                high_half(LAST, 1)
                components(LAST, 0)
                components(LAST, 1)

        @block.tensor
        def _(pe):
            pe.wait_ge(prep, FQ_READY[0])
            for n in range(4):
                t, q0 = n // 2, n % 2 * 2
                for q in range(2):
                    for m in range(CT):
                        last = pe.matmul(BANK[n][:, q * C:(q + 1) * C], wn[:, m, t * P:(t + 1) * P], fq[:, q0 + q, m, :],
                                         start=(m == 0), stop=(m == CT - 1))
                last.then_inc(prep_mm, 1)
            for t in range(CT):
                for q in range(4):
                    for m in range(CT):
                        last = pe.matmul(BANK[4 + t][:, 0:1], fq[:, q, m, t * P:(t + 1) * P],
                                         vec[:, VEC["conv_b"] + m:VEC["conv_b"] + m + 1],
                                         start=(q == 0 and m == 0), stop=(q == 3 and m == CT - 1))
                last.then_inc(prep_mm, 1)
            pe.wait_ge(prep, PREP_DONE[0])

            with pe.Fori(0, B) as b:
                for n in range(8):
                    pe.wait_ge(comp_used[n], 1 + 20 * b)
                def turn_maxima(i, k):
                    pe.wait_ge(tile_max_ready, b * 20 + SLOTS * i + k + 1)
                    for t in range(CT):
                        last = pe.transpose(turned_bank[:, t * P:(t + 1) * P], tile_max[:, t * P:(t + 1) * P], ident[:])
                    last.then_inc(turned, 1)

                def spread_m(i, k):
                    s = b * 20 + SLOTS * i + k
                    pe.wait_ge(chan_max_ready, s + 1)
                    pe.wait_ge(m_row_ready, 1 + s)
                    for t in range(CT):
                        last = pe.transpose(m_bank[:, t * P:(t + 1) * P],
                                            chan_max[:, k, t:t + 1].broadcast_to([P, P]), ident[:])
                    last.then_inc(m_row_done, 1)

                def product_tiles(k, first, end):
                    for r in range(first, end):
                        for t in range(CT):
                            last = pe.matmul(chunk_bank[k % 2][t][:, 0:C + 1], expo[k % 2][:, r, t * P:(t + 1) * P],
                                             rows[k][:, r, :], start=(r == 0), stop=(r == TILES - 1))
                    return last

                def accumulate(i, k):
                    pe.wait_ge(expo_ready, b * 20 + SLOTS * i + k + 1)
                    pe.wait_ge(merged[k % 2], 1 + CT * (b * 10 + before(i, k)))
                    if isinstance(i, int) and i == GROUPS - 1 and k >= SLOTS - 2:
                        last = product_tiles(k, 0, TILES)
                    else:
                        product_tiles(k, 0, TILES // 2)
                        turn_maxima(*after4(i, k, 2))
                        product_tiles(k, TILES // 2, TILES - 1)
                        spread_m(*after4(i, k, 2))
                        last = product_tiles(k, TILES - 1, TILES)
                    last.then_inc(product_done[k % 2], 1)

                for k in range(2):
                    turn_maxima(0, k)
                    spread_m(0, k)
                wait_alone(pe, (area_reset, 2 * b + 2))
                over_chunks(pe, accumulate, S - 2)
                accumulate(GROUPS - 1, SLOTS - 2)
                accumulate(GROUPS - 1, SLOTS - 1)

                def spread_maxima(i, k):
                    s = b * 20 + 2 * i + k
                    pe.wait_ge(keymax_now, 1 + s + 1)
                    pe.wait_ge(spread_used, 1 + s * 3)
                    for j in range(JC):
                        for h in range(CT):
                            n = (j % 2) * C + h * P
                            last = pe.transpose(max_bank[j // 2][:, n:n + P],
                                                key_max_now[k][:, h * JC + j:h * JC + j + 1].broadcast_to([P, P]), ident[:])
                        if j % 2 or j == JC - 1:
                            last.then_inc(spread, 1)

                def attend(i, k):
                    s = b * 20 + 2 * i + k
                    pe.wait_ge(keys_ready, s * 3 + 3)
                    for j in range(JC):
                        for h in range(CT):
                            pe.wait_ge(attn_used[h], 1 + s * JC + j)
                            for t in range(CT):
                                last = pe.matmul(acc[h][:, 0:C + 1], load_ring[k][:, t * JC + j, h * P:(h + 1) * P],
                                                 vq[:, t, :], start=(t == 0), stop=(t == CT - 1))
                            last.then_inc(attn_done[h], 1)

                def product(dst, pairs_, done):
                    n = 0
                    for (a_hi, a_lo), (x_hi, x_lo) in pairs_:
                        for a, x in ((a_hi, x_hi), (a_hi, x_lo), (a_lo, x_hi)):
                            last = pe.matmul(dst, a, x, start=(n == 0), stop=(n == 3 * len(pairs_) - 1))
                            n += 1
                    last.then_inc(done, 1)

                def fuse(i, k):
                    s = b * 20 + 2 * i + k
                    pe.wait_ge(split_ready, 1 + s + 1)
                    for m in range(CT):
                        pe.wait_ge(conv_used[m], 1 + s * 5)
                        cols = slice(m * P, (m + 1) * P)
                        product(conv_bank[m][:, 0:PX],
                                [((g_hi[:, t, q, cols], g_lo[:, t, q, cols]),
                                  (parity(o_hi[k], t, q), parity(o_lo[k], t, q))) for q in range(4) for t in range(CT)],
                                conv_done[m])

                def convolve(i, k, m):
                    s = b * 20 + 2 * i + k
                    cols = slice(m * P, (m + 1) * P)
                    for n in range(4):
                        q = n % 2 * 2 + n // 2
                        pe.wait_ge(conv_used[n % 2], 1 + s * 5 + 1 + 2 * m + n // 2)
                        product(conv_bank[n % 2][:, 0:PX],
                                [((w_hi[:, t, cols], w_lo[:, t, cols]),
                                  (parity(o_hi[k], t, q), parity(o_lo[k], t, q))) for t in range(CT)],
                                conv_done[n % 2])

                def turn(i, k, n):
                    s = b * 20 + 2 * i + k
                    for t in range(CT):
                        pe.wait_ge(conv_used[t], 1 + s * 5 + 1)
                    pe.wait_ge(px_used, 1 + 2 * s + n)
                    for r in range(2):
                        for t in range(CT):
                            px = (2 * n + r) * W2
                            last = pe.transpose(px_bank[0:W2, r * C + t * P:r * C + (t + 1) * P],
                                                fused_now[k][:, t, px:px + W2], ident[:])
                    last.then_inc(px_done, 1)

                def conv_stage(i, k):
                    fuse(i, k)
                    convolve(i, k, 0)
                    turn(i, k, 0)
                    convolve(i, k, 1)
                    turn(i, k, 1)

                pe.wait_ge(m_row_ready, 1 + 20 * b + 20)
                spread_maxima(0, 0)
                pe.wait_ge(vq_scaled, 2 * b + 2)
                for t in range(CT):
                    for d in range(CT):
                        last = pe.transpose(conv_bank[t][:, d * P:(d + 1) * P], vqT[:, d, t * P:(t + 1) * P], ident[:])
                last.then_inc(vq_turned, 1)
                spread_maxima(0, 1)
                pe.wait_ge(vq_ready, 2 * b + 2)
                attend(0, 0)
                with pe.Fori(0, LAST) as i:
                    for k in range(2):
                        spread_maxima(i + 1, k)
                        attend(*after(i, k, 1))
                        conv_stage(i, k)
                attend(LAST, 1)
                conv_stage(LAST, 0)
                conv_stage(LAST, 1)

                pe.wait_ge(maps_ready, b + 1)
                for m in range(2):
                    for ky in range(KS):
                        last = pe.matmul(BANK[4][0:H2, 0:W2], maps[:, m, ky:ky + H2], band[:, m * KS + ky, :],
                                         start=(m == 0 and ky == 0), stop=(m == 1 and ky == KS - 1))
                last.then_inc(att_done, 1)
                pe.wait_ge(stats_ready, 2 * b + 2)
                for t in range(CT):
                    last = pe.matmul(BANK[5][0:HID, 0:2], w1[:, t, :], stats[:, t, :], start=(t == 0), stop=(t == CT - 1))
                last.then_inc(mlp1_done, 1)
                pe.wait_ge(mlp1_ready, b + 1)
                for t in range(CT):
                    last = pe.matmul(BANK[6][:, t:t + 1], w2[:, t * P:(t + 1) * P], hidden_sum[:], start=True, stop=True)
                last.then_inc(mlp2_done, 1)

                wait_alone(pe, (gate_exp, b + 1), (proj_ready, 2 * b + 2))
                wait_alone(pe, (conv_used[0], 100 * b + 100), (conv_used[1], 100 * b + 100))
                with pe.Fori(0, S // 2) as i:
                    for k in range(2):
                        s = b * 20 + 2 * i + k
                        pe.wait_ge(s_ready, 1 + s + 1)
                        for n in range(8):
                            pe.wait_ge(comp_used[n], 1 + s)
                            cols = slice(n * P, (n + 1) * P)
                            for m, (a, x) in enumerate((a, x) for t in range(CT) for a, x in (
                                    (p_hi[:, t, cols], s_hi[k][:, t, :]), (p_hi[:, t, cols], s_lo[k][:, t, :]),
                                    (p_lo[:, t, cols], s_hi[k][:, t, :]))):
                                last = pe.matmul(BANK[n][:, 0:PX], a, x, start=(m == 0), stop=(m == 5))
                            last.then_inc(comp_done[n], 1)


def kernel(x, L0_conv_conv_w, L0_conv_conv_b, L0_conv_gamma, L1_conv_fusion_w, L1_conv_fusion_b, L1_conv_bn1_g,
           L1_conv_bn1_b, L1_conv_bn1_m, L1_conv_bn1_v, L1_conv_sa_w, L1_conv_ca_w1, L1_conv_ca_w2, L1_conv_proj_w,
           L1_conv_proj_b, L1_conv_bn2_g, L1_conv_bn2_b, L1_conv_bn2_m, L1_conv_bn2_v):
    import concourse.bacc as bacc
    from concourse.bass_utils import run_bass_kernel_spmd

    x = np.asarray(x)
    B = x.shape[0]
    blocks = x.reshape(B, CT, P, CT, P, S, JC)
    x_rows = blocks.transpose(0, 5, 4, 3, 6, 1, 2).reshape(B, S, P, CT * POS)
    x_keys = blocks.transpose(0, 5, 2, 1, 6, 3, 4).reshape(B, S, P, CT * POS)
    x_pos = x.reshape(B, CT, P, S, ROWS, W2, 2).transpose(0, 3, 2, 1, 6, 4, 5).reshape(B, S, P, CT * POS)

    def columns(v):
        return np.asarray(v).reshape(-1, P).T

    vectors = np.concatenate([columns(v) for v in (
        L0_conv_conv_b, L1_conv_fusion_b, L1_conv_bn1_g, L1_conv_bn1_b, L1_conv_bn1_m, L1_conv_bn1_v, L1_conv_proj_b,
        L1_conv_bn2_g, L1_conv_bn2_b, L1_conv_bn2_m, L1_conv_bn2_v)], axis=1)
    sa = np.asarray(L1_conv_sa_w)[0]
    bands = np.zeros((W2, 2 * KS, W2), sa.dtype)
    for m in range(2):
        for ky in range(KS):
            for w_out in range(W2):
                for kx in range(KS):
                    w_in = w_out + kx - PAD
                    if 0 <= w_in < W2:
                        bands[w_in, m * KS + ky, w_out] = sa[m, ky, kx]

    arrays = {
        "x_rows": x_rows, "x_keys": x_keys, "x_pos": x_pos, "conv_w": np.asarray(L0_conv_conv_w),
        "conv_wT": np.asarray(L0_conv_conv_w).T, "fusion_wT": np.asarray(L1_conv_fusion_w).T,
        "proj_wT": np.asarray(L1_conv_proj_w).T, "w1T": np.asarray(L1_conv_ca_w1).T,
        "w2T": np.asarray(L1_conv_ca_w2).T, "vectors": vectors, "gamma": np.asarray(L0_conv_gamma), "bands": bands,
        "identity": np.eye(P, dtype=np.float32),
    }
    arrays = {f"in_{k}": np.ascontiguousarray(v) for k, v in arrays.items()}
    nc = bacc.Bacc("TRN2", target_bir_lowering=False, num_devices=1)
    args = [nc.dram_tensor(k, v.shape, mybir.dt.from_np(v.dtype), kind="ExternalInput").ap() for k, v in arrays.items()]
    out = nc.dram_tensor("out", (B, S, P, CT * POS), F32, kind="ExternalOutput").ap()
    build(nc, B, *args, out)
    got = run_bass_kernel_spmd(nc, [arrays], core_ids=[0]).results[0]["out"]
    return np.ascontiguousarray(got.reshape(B, S, P, CT, 2, 2, HR, W2).transpose(0, 3, 2, 1, 6, 5, 7, 4)).reshape(B, C, H, W)
```

```python
from contextlib import ExitStack

import numpy as np

import concourse.bass as bass
from concourse import mybir

F32 = mybir.dt.float32
F32R = mybir.dt.float32r
ACT = mybir.ActivationFunctionType
ALU = mybir.AluOpType
AX = mybir.AxisListType

P = 128
C = 256
CT = C // P
H = W = 160
N = H * W
J = N // C
JC = 5
S = J // JC
POS = JC * C
ROWS = POS // W
W2 = W // 2
H2 = H // 2
HR = ROWS // 2
PX = HR * W2
HALF = POS // 2
PXS = H2 * W2
HID = C // 16
KS = 7
PAD = KS // 2
EPS = 1e-5
TILES = JC * CT
SLOTS = 4
LOADS = S // SLOTS + 2 * (S // 2)
LOWEST = -3.0e38
VEC = {"conv_b": 0, "fusion_b": 2, "bn1_g": 4, "bn1_b": 6, "bn1_m": 8, "bn1_v": 10,
       "proj_b": 12, "bn2_g": 20, "bn2_b": 28, "bn2_m": 36, "bn2_v": 44}
NVEC = 52


def build(nc, B, x_rows, x_keys, x_pos, conv_w, conv_wT, fusion_wT, proj_wT, w1T, w2T, vectors, gamma, bands,
          identity, out):
    y_dram = nc.dram_tensor("y_scratch", [B, S, P, CT * POS], F32).ap()
    sig_dram = nc.dram_tensor("sig_scratch", [B, H2, W2], F32).ap()

    FQ_READY, VAR_READY, PREP_DONE = [0], [0], [0]

    with ExitStack() as ctx:
        def sb(name, shape, dt=F32, stack=ctx):
            return stack.enter_context(nc.sbuf_tensor(name, shape, dt))

        def sem(name):
            return ctx.enter_context(nc.semaphore(name))

        def sems(name, n):
            return [sem(f"{name}{i}") for i in range(n)]

        ident = sb("ident", [P, P])
        vec = sb("vec", [P, NVEC])
        gam = sb("gam", [P, 1])
        w_hi = sb("w_hi", [P, CT, C], F32R)
        w_lo = sb("w_lo", [P, CT, C], F32R)
        g_hi = sb("g_hi", [P, CT, 4, C], F32R)
        g_lo = sb("g_lo", [P, CT, 4, C], F32R)
        proj = sb("proj", [P, CT, 4 * C])
        w1 = sb("w1", [P, CT, HID])
        w2 = sb("w2", [HID, C])
        band = sb("band", [W2, 2 * KS, W2])
        scale1 = sb("scale1", [P, CT])
        bias1 = sb("bias1", [P, CT])
        scale2 = sb("scale2", [P, 8])
        bias2 = sb("bias2", [P, 8])
        small = sb("small", [P, 16])
        unused = sb("unused", [P, 1])

        load_ring = [sb(f"load_ring{k}", [P, TILES, C + 1]) for k in range(2)]
        fused = sb("fused", [P, CT, PXS])
        chunk_max = sb("chunk_max", [P, CT])
        chan_max = sb("chan_max", [P, SLOTS, CT])
        rescale = sb("rescale", [P, SLOTS, CT])
        key_max = sb("key_max", [P, S, TILES])
        key_max_now = [sb(f"key_max_now{k}", [P, TILES]) for k in range(2)]
        vq_sum = sb("vq_sum", [P, CT])
        vq_scale = sb("vq_scale", [P, CT])
        vqT = sb("vqT", [P, CT, C + 1])
        vq_hi = sb("vq_hi", [P, CT, C + 2], F32R)
        vq_lo = sb("vq_lo", [P, CT, C + 2], F32R)
        attn_inv = sb("attn_inv", [P, 2, CT])
        maps = sb("maps", [W2, 2, H2 + 2 * PAD])
        part_max = sb("part_max", [P, CT, JC])
        part_sum = sb("part_sum", [P, CT, JC])
        stats = sb("stats", [P, CT, 2])
        hidden = sb("hidden", [HID, 2])
        hidden_sum = sb("hidden_sum", [HID, 1])
        chan_gate = sb("chan_gate", [P, CT])

        with ExitStack() as area:
            expo = [sb(f"expo{k}", [P, TILES, C], F32, area) for k in range(2)]
            late_rows = sb("late_rows", [P, TILES, C + 1], F32, area)
            tile_max = sb("tile_max", [P, C], F32, area)
            m_row = [sb(f"m_row{k}", [P, C], F32, area) for k in range(2)]
            fT = sb("fT", [P, 4, CT, C], F32, area)
            fq = sb("fq", [P, 4, CT, C], F32, area)
            ftmp = sb("ftmp", [P, 4, CT, C], F32, area)
            wn = sb("wn", [P, CT, C], F32, area)
            wt = sb("wt", [P, CT, C], F32, area)
        with ExitStack() as area:
            out2 = [sb(f"out2_{k}", [P, CT, POS], F32, area) for k in range(2)]
            o_hi = [sb(f"o_hi{k}", [P, CT, POS], F32R, area) for k in range(2)]
            o_lo = [sb(f"o_lo{k}", [P, CT, POS], F32R, area) for k in range(2)]
            y_out = [sb(f"y_out{k}", [P, POS], F32, area) for k in range(CT)]
            fused_now = [sb(f"fused_now{k}", [P, CT, PX], F32, area) for k in range(2)]
            key_hi = sb("key_hi", [P, TILES, C], F32R, area)
            key_lo = sb("key_lo", [P, TILES, C], F32R, area)
        with ExitStack() as area:
            s_hi = [sb(f"s_hi{k}", [P, CT, PX], F32R, area) for k in range(2)]
            s_lo = [sb(f"s_lo{k}", [P, CT, PX], F32R, area) for k in range(2)]
            p_hi = sb("p_hi", [P, CT, 4 * C], F32R, area)
            p_lo = sb("p_lo", [P, CT, 4 * C], F32R, area)
            with ExitStack() as sub:
                sig = sb("sig", [H2, W2], F32, sub)
                sig_all = sb("sig_all", [P, PXS], F32, sub)
                junk = sb("junk", [P, 4 * PX], F32, sub)
            with ExitStack() as sub:
                comp = [sb(f"comp{k}", [P, CT, 4, PX], F32, sub) for k in range(2)]
                pairs = sb("pairs", [P, CT, 4, PX], F32, sub)
                result = [sb(f"result{k}", [P, CT, 4, PX], F32, sub) for k in range(2)]
                early_rows = sb("early_rows", [P, TILES, C + 1], F32, sub)

        psum = ctx.enter_context(nc.psum_tensor("psum", [P, 8, 512], F32))
        BANK = [psum[:, i, :] for i in range(8)]
        chunk_bank = (BANK[0:2], BANK[2:4])
        turned_bank = BANK[4]
        m_bank = BANK[5]
        acc = (psum[:, 0:2, :], psum[:, 4:6, :])
        conv_bank = BANK[2:4]
        max_bank = BANK[4:7]
        px_bank = BANK[7]

        fusion_loaded = sem("fusion_loaded")
        weights_loaded = sem("weights_loaded")
        ring_loaded = sems("ring_loaded", 2)
        early_loaded = sem("early_loaded")
        late_loaded = sem("late_loaded")
        pos_loaded = sems("pos_loaded", 2)
        sig_loaded = sems("sig_loaded", JC)
        y_stored = sems("y_stored", 2)
        out_stored = sems("out_stored", 2)
        sig_stored = sem("sig_stored")
        prep = sem("prep")
        prep_mm = sem("prep_mm")
        passed = sem("passed")
        prep_root = sem("prep_root")
        area_reset = sem("area_reset")
        reset = sem("reset")
        tile_max_ready = sem("tile_max_ready")
        turned = sem("turned")
        max_steps = sem("max_steps")
        chan_max_ready = sem("chan_max_ready")
        m_row_done = sem("m_row_done")
        m_row_ready = sem("m_row_ready")
        rescale_ready = sem("rescale_ready")
        keymax_ready = sem("keymax_ready")
        shifted = sems("shifted", 2)
        expo_ready = sem("expo_ready")
        product_done = sems("product_done", 2)
        merged = sems("merged", 2)
        vq_steps = sem("vq_steps")
        vq_scaled = sem("vq_scaled")
        vq_turned = sem("vq_turned")
        vq_hi_ready = sem("vq_hi_ready")
        vq_ready = sem("vq_ready")
        keymax_now = sem("keymax_now")
        spread = sem("spread")
        spread_used = sem("spread_used")
        keys_exp = sem("keys_exp")
        key_hi_ready = sem("key_hi_ready")
        keys_ready = sem("keys_ready")
        attn_done = sems("attn_done", 2)
        attn_used = [sems(f"attn_used{n}_", 2) for n in range(2)]
        inv_ready = sem("inv_ready")
        hi_ready = sem("hi_ready")
        split_ready = sem("split_ready")
        conv_done = sems("conv_done", 2)
        conv_used = sems("conv_used", 2)
        fused_kept = sem("fused_kept")
        px_done = sem("px_done")
        px_used = sem("px_used")
        maps_ready = sem("maps_ready")
        att_done = sem("att_done")
        att_exp = sem("att_exp")
        att_steps = sem("att_steps")
        sig_ready = sem("sig_ready")
        gated = sem("gated")
        summed = sem("summed")
        stat_steps = sem("stat_steps")
        stats_ready = sem("stats_ready")
        mlp1_done = sem("mlp1_done")
        mlp1_ready = sem("mlp1_ready")
        mlp2_done = sem("mlp2_done")
        gate_exp = sem("gate_exp")
        gate_steps = sem("gate_steps")
        proj_hi_ready = sem("proj_hi_ready")
        proj_ready = sem("proj_ready")
        s_hi_ready = sem("s_hi_ready")
        s_ready = sem("s_ready")
        comp_done = sems("comp_done", 8)
        comp_used = sems("comp_used", 8)
        pairs_ready = sem("pairs_ready")
        haar_done = sems("haar_done", 2)
        added = sems("added", 2)

        block = ctx.enter_context(nc.Block())

        def slot(k):
            return load_ring[k][:, :, 0:C]

        def slot4(k):
            return slot(k).rearrange("p (t r) c -> p t r c", t=CT)

        key_hi4 = key_hi[:].rearrange("p (t r) c -> p t r c", t=CT)
        key_lo4 = key_lo[:].rearrange("p (t r) c -> p t r c", t=CT)

        def piece_of(tiles, n):
            return tiles[:, :, 2 * n:min(2 * n + 2, JC), :]

        def block_of(tile, t, j):
            return tile[:, t, :].rearrange("p (w n) -> p w n", w=2)[:, :, j * P:(j + 1) * P]

        def parity(tile, t, q):
            half = tile[:, t, q % 2 * HALF:(q % 2 + 1) * HALF]
            return half.rearrange("p (h a w) -> p h a w", a=2, w=W2)[:, :, q // 2, :]

        def at(v, b, s):
            return v[bass.ds(b, 1), bass.ds(s, 1)].rearrange("b s p n -> p (b s n)")

        def at_t(v, b, t, s):
            return at(v, b, s)[:, t * POS:(t + 1) * POS]

        def after(i, k, n):
            return i + (k + n) // 2, (k + n) % 2

        def blocks_before(k, j):
            return (k * JC + j) // 2

        def blocks_after(k, n):
            return ((k + 1) * JC + 1 - n) // 2

        def is_chunk(i, k):
            return not isinstance(i, int) or 2 * i + k < S

        def stage2(eng, step):
            with eng.Fori(0, S // 2 - 2) as i:
                for k in range(2):
                    step(i, k)
            for s in range(S - 4, S):
                step(s // 2, s % 2)

        LAST = S // 2 - 1
        PIECES = 3

        rows = [early_rows, *load_ring, late_rows]
        rows_loaded = [early_loaded, *ring_loaded, late_loaded]
        GROUPS = S // SLOTS

        def x_rows_of(k):
            return rows[k][:, :, 0:C]

        def before(i, k):
            return 2 * i + k // 2

        def rows_in(b, i, k):
            return (b * (LOADS if k in (1, 2) else GROUPS) + i + 1) * 16

        def after4(i, k, n):
            return i + (k + n) // SLOTS, (k + n) % SLOTS

        def over_chunks(eng, step, last):
            with eng.Fori(0, last // SLOTS) as i:
                for k in range(SLOTS):
                    step(i, k)
            for k in range(last % SLOTS):
                step(last // SLOTS, k)

        def wait_alone(eng, *waits):
            for semaphore, value in waits:
                eng.wait_ge(semaphore, value + (1 if semaphore in FROM_ONE else 0))
                eng.sem_inc(passed, 1)

        FROM_ONE = [keymax_now, split_ready, px_done, px_used, fused_kept, spread_used, summed, s_ready, m_row_ready]
        for group in (shifted, product_done, merged, haar_done, attn_done, *attn_used, conv_done, conv_used, comp_done,
                      comp_used, added, y_stored, out_stored):
            FROM_ONE += group

        @block.sync
        def _(sp):
            tiled = "(t p) o -> p t o"
            sp.dma_start(fT[:], fusion_wT.rearrange("(q t p) o -> p q t o", q=4, p=P)).then_inc(fusion_loaded, 16)
            for dst, src in ((wn[:], conv_w.rearrange(tiled, p=P)), (vec[:], vectors), (ident[:], identity),
                             (gam[:], gamma.rearrange("(a n) -> a n", a=1).broadcast_to([P, 1])),
                             (wt[:], conv_wT.rearrange(tiled, p=P)),
                             (proj[:], proj_wT.rearrange(tiled, p=P)), (w1[:], w1T.rearrange(tiled, p=P)),
                             (w2[:], w2T), (band[:], bands)):
                sp.dma_start(dst, src).then_inc(weights_loaded, 16)

            def rows_at(n):
                return x_rows[bass.ds(n, 1)].rearrange("s p n -> p (s n)")

            sp.dma_start(x_rows_of(0), rows_at(0)).then_inc(early_loaded, 16)
            sp.dma_start(x_rows_of(1), rows_at(1)).then_inc(ring_loaded[0], 16)
            with sp.Fori(0, B) as b:
                def load_rows(i, k):
                    sp.dma_start(x_rows_of(k), rows_at(b * S + SLOTS * i + k)).then_inc(rows_loaded[k], 16)

                wait_alone(sp, (added[1], b * 10))
                load_rows(0, 2)
                wait_alone(sp, (haar_done[0], b * 10), (haar_done[1], b * 10), (comp_done[7], b * 20))
                load_rows(0, 3)
                with sp.Fori(1, GROUPS) as i:
                    for k in range(SLOTS):
                        wait_alone(sp, (product_done[k % 2], b * 10 + before(i, k) - 1),
                                   (keymax_ready, b * 20 + SLOTS * (i - 1) + k + 1))
                        load_rows(i, k)

                def chunks_before(i, k):
                    return b * 20 if isinstance(i, int) and i == 0 else b * 20 + 2 * i + k - 1

                def load_keys(i, k):
                    sp.wait_ge(attn_done[1], 1 + chunks_before(i, k) * JC)
                    sp.dma_start(slot(k), at(x_keys, b, 2 * i + k)).then_inc(ring_loaded[k], 16)

                def load_pos(i, k):
                    sp.wait_ge(split_ready, 1 + chunks_before(i, k))
                    sp.dma_start(out2[k][:].rearrange("p t n -> p (t n)"), at(x_pos, b, 2 * i + k)).then_inc(pos_loaded[k], 16)

                def store_y(i, k):
                    s = b * 20 + 2 * i + k
                    for t in range(CT):
                        wait_alone(sp, (conv_used[0], s * 5 + 3 + 2 * t), (conv_used[1], s * 5 + 3 + 2 * t))
                        sp.dma_start(at_t(y_dram, b, t, 2 * i + k), y_out[t][:]).then_inc(y_stored[t], 16)

                wait_alone(sp, (product_done[1], b * 10 + 9), (keymax_ready, b * 20 + 18))
                load_keys(0, 0)
                wait_alone(sp, (product_done[0], b * 10 + 10), (keymax_ready, b * 20 + 19))
                load_keys(0, 1)
                wait_alone(sp, (product_done[0], b * 10 + 10), (product_done[1], b * 10 + 10),
                           (keymax_ready, b * 20 + 20), (out_stored[0], b * 160), (out_stored[1], b * 160))
                for k in range(2):
                    load_pos(0, k)
                load_keys(1, 0)

                def chunk(i, k):
                    if is_chunk(*after(i, k, 2)):
                        load_pos(*after(i, k, 2))
                    if is_chunk(*after(i, k, 3)):
                        load_keys(*after(i, k, 3))
                    store_y(i, k)

                stage2(sp, chunk)
                wait_alone(sp, (y_stored[0], 320 * b + 320), (y_stored[1], 320 * b + 320))

                sp.wait_ge(sig_ready, b + 1)
                sp.dma_start(sig_dram[bass.ds(b, 1)].rearrange("b h w -> h (b w)"), sig[:]).then_inc(sig_stored, 16)
                sp.wait_ge(sig_stored, 16 * b + 16)
                n = PXS // JC
                for q in range(JC):
                    sp.dma_start(sig_all[:, q * n:(q + 1) * n], sig_dram[bass.ds(b, 1)].rearrange(
                        "b h w -> b (h w)")[:, q * n:(q + 1) * n].broadcast_to([P, n])).then_inc(sig_loaded[q], 16)

                def load_y(i, k):
                    sp.dma_start(slot(k), at(y_dram, b, 2 * i + k)).then_inc(ring_loaded[k], 16)

                def store_out(i, k):
                    sp.wait_ge(added[k], 1 + b * 10 + i + 1)
                    sp.dma_start(at(out, b, 2 * i + k), result[k][:].rearrange("p t a n -> p (t a n)")).then_inc(
                        out_stored[k], 16)

                for k in range(2):
                    sp.wait_ge(attn_done[1], 1 + (b * 20 + 20) * JC)
                    load_y(0, k)
                sp.dma_start(x_rows_of(0), rows_at(b * S + S)).then_inc(early_loaded, 16)
                with sp.Fori(0, LAST) as i:
                    for k in range(2):
                        store_out(i, k)
                        load_y(i + 1, k)
                store_out(LAST, 0)
                sp.dma_start(x_rows_of(1), rows_at(b * S + S + 1)).then_inc(ring_loaded[0], 16)
                store_out(LAST, 1)
            for k in range(2):
                sp.wait_ge(out_stored[k], 1 + 160 * B)
            sp.wait_ge(early_loaded, (B * GROUPS + 1) * 16)
            sp.wait_ge(ring_loaded[0], (B * LOADS + 1) * 16)

        @block.vector
        def _(dve):
            steps = [0]

            def step(ins):
                steps[0] += 1
                ins.then_inc(prep, 1)
                dve.wait_ge(prep, steps[0])

            def col(name, n=CT):
                return vec[:, VEC[name]:VEC[name] + n]

            step(dve.memset(small[:, 0:2], 1.0))
            for t in range(CT):
                step(dve.tensor_copy(vq_hi[:, t, C:C + 2], small[:, 0:2]))
                step(dve.tensor_tensor(vq_lo[:, t, C:C + 2], small[:, 0:2], small[:, 0:2], ALU.subtract))
            dve.memset(load_ring[0][:, :, C:C + 1], 1.0)
            dve.memset(load_ring[1][:, :, C:C + 1], 1.0)
            step(dve.memset(maps[:], 0.0))
            dve.wait_ge(fusion_loaded, 16)
            step(dve.tensor_tensor(ftmp[:, 0:2], fT[:, 0:3:2], fT[:, 1:4:2], ALU.add))
            step(dve.tensor_tensor(ftmp[:, 2:4], fT[:, 0:3:2], fT[:, 1:4:2], ALU.subtract))
            for n in range(2):
                step(dve.tensor_tensor(fq[:, 2 * n], ftmp[:, 2 * n], ftmp[:, 2 * n + 1], ALU.add))
                step(dve.tensor_tensor(fq[:, 2 * n + 1], ftmp[:, 2 * n], ftmp[:, 2 * n + 1], ALU.subtract))
            FQ_READY[0] = steps[0]
            dve.wait_ge(weights_loaded, 144)
            step(dve.tensor_scalar(small[:, 0:2], col("bn1_v"), EPS, None, ALU.add))
            step(dve.tensor_scalar(small[:, 2:10], col("bn2_v", 8), EPS, None, ALU.add))
            VAR_READY[0] = steps[0]
            step(dve.tensor_copy(w_hi[:], wt[:]))
            step(dve.tensor_tensor(w_lo[:], wt[:], w_hi[:].bitcast(F32), ALU.subtract))
            dve.wait_ge(prep_root, 1)
            step(dve.reciprocal(small[:, 0:10], small[:, 0:10]))
            step(dve.tensor_tensor(scale1[:], small[:, 0:2], col("bn1_g"), ALU.mult))
            step(dve.tensor_tensor(scale2[:], small[:, 2:10], col("bn2_g", 8), ALU.mult))
            step(dve.tensor_tensor(bias2[:], col("proj_b", 8), col("bn2_m", 8), ALU.subtract))
            step(dve.tensor_tensor(bias2[:], bias2[:], scale2[:], ALU.mult))
            step(dve.tensor_tensor(bias2[:], bias2[:], col("bn2_b", 8), ALU.add))
            step(dve.tensor_scalar(bias2[:], bias2[:], 0.5, None, ALU.mult))
            step(dve.tensor_scalar(scale2[:], scale2[:], 0.5, None, ALU.mult))
            for n in range(4):
                t, q = n // 2, n % 2 * 2
                dve.wait_ge(prep_mm, n + 1)
                src = BANK[n][:].rearrange("p (q o) -> p q o", q=2)
                step(dve.tensor_copy(g_hi[:, t, q:q + 2, :], src))
                step(dve.tensor_tensor(g_lo[:, t, q:q + 2, :], src, g_hi[:, t, q:q + 2, :].bitcast(F32), ALU.subtract))
            dve.wait_ge(prep_mm, 6)
            for t in range(CT):
                step(dve.tensor_scalar(small[:, 10 + t:11 + t], BANK[4 + t][:, 0:1], 0.5, None, ALU.mult))
            step(dve.tensor_tensor(bias1[:], small[:, 10:12], col("fusion_b"), ALU.add))
            step(dve.tensor_tensor(bias1[:], bias1[:], col("bn1_m"), ALU.subtract))
            step(dve.tensor_tensor(bias1[:], bias1[:], scale1[:], ALU.mult))
            step(dve.tensor_tensor(bias1[:], bias1[:], col("bn1_b"), ALU.add))
            step(dve.tensor_scalar(scale1[:], scale1[:], 0.5, None, ALU.mult))
            PREP_DONE[0] = steps[0]

            with dve.Fori(0, B) as b:
                dve.memset(chan_max[:, SLOTS - 1, :], LOWEST).then_inc(reset, 1)
                dve.memset(vqT[:], 0.0).then_inc(reset, 1)
                dve.wait_ge(reset, 2 * b + 2)
                wait_alone(dve, (keymax_now, 20 * b))

                def maxima(i, k):
                    s = b * 20 + SLOTS * i + k
                    dve.wait_ge(rows_loaded[k], rows_in(b, i, k))
                    dve.tensor_reduce(tile_max[:], x_rows_of(k).rearrange("p r c -> p c r"), AX.X, ALU.max).then_inc(
                        tile_max_ready, 1)
                    dve.wait_ge(turned, s + 1)
                    dve.tensor_reduce(chunk_max[:], turned_bank[:, 0:C].rearrange("p (t n) -> p t n", t=CT), AX.X,
                                      ALU.max).then_inc(max_steps, 1)
                    dve.wait_ge(max_steps, 2 * s + 1)
                    m_before = chan_max[:, (k - 1) % SLOTS, :]
                    dve.tensor_tensor(chan_max[:, k, :], m_before, chunk_max[:], ALU.max).then_inc(chan_max_ready, 1)
                    dve.wait_ge(chan_max_ready, s + 1)
                    dve.tensor_tensor(rescale[:, k, :], m_before, chan_max[:, k, :], ALU.subtract).then_inc(max_steps, 1)

                def key_maxima(i, k):
                    dve.tensor_reduce(key_max[:, bass.ds(SLOTS * i + k, 1), :].rearrange("p s t -> p (s t)"),
                                      x_rows_of(k), AX.X, ALU.max).then_inc(keymax_ready, 1)

                def merge(i, k):
                    s = b * 20 + SLOTS * i + k
                    dve.wait_ge(rescale_ready, s + 1)
                    dve.wait_ge(product_done[k % 2], 1 + b * 10 + before(i, k) + 1)
                    dve.wait_ge(merged[(k + 1) % 2], 1 + CT * (b * 10 + 2 * i + (k + 1) // 2))
                    for t in range(CT):
                        dve.scalar_tensor_tensor(out=vqT[:, t, :], in0=vqT[:, t, :], scalar=rescale[:, k, t:t + 1],
                                                 in1=chunk_bank[k % 2][t][:, 0:C + 1], op0=ALU.mult,
                                                 op1=ALU.add).then_inc(merged[k % 2], 1)

                def shift_keys(i, k):
                    s = b * 20 + 2 * i + k
                    dve.wait_ge(ring_loaded[k], (b * LOADS + GROUPS + i + 1) * 16)
                    for n in range(PIECES):
                        dve.wait_ge(spread, s * PIECES + n + 1)
                        r = min(2, JC - 2 * n)
                        piece = slot4(k)[:, :, 2 * n:2 * n + r, :]
                        dve.tensor_tensor(piece, piece, max_bank[n][:, 0:r * C].rearrange(
                            "p (a r c) -> p a r c", a=1, c=C).broadcast_to([P, CT, r, C]),
                            ALU.subtract).then_inc(spread_used, 1)

                maxima(0, 0)
                maxima(0, 1)
                key_maxima(0, 0)
                key_maxima(0, 1)

                def both(i, k):
                    maxima(*after4(i, k, 2))
                    key_maxima(*after4(i, k, 2))
                    merge(i, k)

                over_chunks(dve, both, S - 2)
                merge(GROUPS - 1, SLOTS - 2)
                shift_keys(0, 0)
                shift_keys(0, 1)
                merge(GROUPS - 1, SLOTS - 1)

                for k in range(2):
                    dve.wait_ge(merged[k], 1 + CT * (b * 10 + 10))
                dve.reciprocal(vq_sum[:], vqT[:, :, C]).then_inc(vq_steps, 1)
                dve.wait_ge(vq_steps, 2 * b + 1)
                dve.tensor_scalar(vq_scale[:], vq_sum[:], gam[:, 0:1], None, ALU.mult).then_inc(vq_steps, 1)
                dve.wait_ge(vq_steps, 2 * b + 2)
                for t in range(CT):
                    dve.tensor_scalar(vqT[:, t, 0:C], vqT[:, t, 0:C], vq_scale[:, t:t + 1], None, ALU.mult).then_inc(
                        vq_scaled, 1)

                def add_attention(i, k):
                    s = b * 20 + 2 * i + k
                    dve.wait_ge(pos_loaded[k], (b * 10 + i + 1) * 16)
                    for j in range(JC):
                        n = (k + j) % 2
                        for t in range(CT):
                            dve.wait_ge(attn_done[t], 1 + s * JC + j + 1)
                        dve.reciprocal(attn_inv[:, n, :], acc[n][:, :, C]).then_inc(inv_ready, 1)
                        dve.wait_ge(inv_ready, s * JC + j + 1)
                        for t in range(CT):
                            o = block_of(out2[k], t, j)
                            dve.scalar_tensor_tensor(out=o, in0=acc[n][:, t, 0:C].rearrange("p (w n) -> p w n", w=2),
                                                     scalar=attn_inv[:, n, t:t + 1], in1=o, op0=ALU.mult,
                                                     op1=ALU.add).then_inc(attn_used[n][t], 1)

                def split(i, k):
                    s = b * 20 + 2 * i + k
                    for n in range(2):
                        for t in range(CT):
                            dve.wait_ge(attn_used[n][t], 1 + (b * 10 + i) * JC + blocks_after(k, n))
                    dve.wait_ge(conv_done[1], 1 + ((b * 20 if isinstance(i, int) and i == 0 else s - 1) * 5))
                    dve.tensor_copy(o_hi[k][:], out2[k][:]).then_inc(hi_ready, 1)
                    dve.wait_ge(hi_ready, s + 1)
                    dve.tensor_tensor(o_lo[k][:], out2[k][:], o_hi[k][:].bitcast(F32), ALU.subtract).then_inc(
                        split_ready, 1)

                def map_rows(i, k, n):
                    s = b * 20 + 2 * i + k
                    dve.wait_ge(px_done, 1 + 2 * s + n + 1)
                    src = px_bank[0:W2, :].rearrange("p (r c) -> p r c", c=C)
                    at_row = (2 * i + k) * HR + 2 * n + PAD
                    dve.tensor_reduce(maps[:, 1, bass.ds(at_row, 2)], src, AX.X, ALU.max)
                    dve.tensor_reduce(maps[:, 0, bass.ds(at_row, 2)], src, AX.X, ALU.add).then_inc(px_used, 1)

                dve.wait_ge(vq_turned, b + 1)
                for t in range(CT):
                    turned_vq = conv_bank[t][:, 0:C].rearrange("p (n w) -> p w n", w=2)
                    hi = vq_hi[:, t, 0:C].rearrange("p (w n) -> p w n", w=2)
                    dve.tensor_copy(hi, turned_vq).then_inc(vq_hi_ready, 1)
                    dve.wait_ge(vq_hi_ready, CT * b + t + 1)
                    dve.tensor_tensor(vq_lo[:, t, 0:C].rearrange("p (w n) -> p w n", w=2), turned_vq, hi.bitcast(F32),
                                      ALU.subtract).then_inc(vq_ready, 1)
                add_attention(0, 0)
                split(0, 0)
                shift_keys(1, 0)

                def chunk(i, k):
                    if is_chunk(*after(i, k, 1)):
                        add_attention(*after(i, k, 1))
                        split(*after(i, k, 1))
                    map_rows(i, k, 0)
                    if is_chunk(*after(i, k, 3)):
                        shift_keys(*after(i, k, 3))
                    map_rows(i, k, 1)

                stage2(dve, chunk)

                dve.wait_ge(px_used, 1 + 40 * b + 40)
                dve.tensor_scalar(maps[:, 0, PAD:PAD + H2], maps[:, 0, PAD:PAD + H2], 1.0 / C, None, ALU.mult).then_inc(
                    maps_ready, 1)
                dve.wait_ge(att_exp, b + 1)
                dve.tensor_scalar(sig[:], sig[:], 1.0, None, ALU.add).then_inc(att_steps, 1)
                dve.wait_ge(att_steps, b + 1)
                dve.reciprocal(sig[:], sig[:]).then_inc(sig_ready, 1)
                wait_alone(dve, (fused_kept, 20 * b + 20))
                n = PXS // JC
                for q in range(JC):
                    wait_alone(dve, (sig_loaded[q], 16 * b + 16))
                    for t in range(CT):
                        f = fused[:, t, q * n:(q + 1) * n]
                        dve.tensor_tensor_reduce(f, f, sig_all[:, q * n:(q + 1) * n], 1.0, 0.0, ALU.mult, ALU.max,
                                                 part_max[:, t, q:q + 1]).then_inc(gated, 1)
                dve.wait_ge(gated, 10 * b + 10)
                dve.tensor_reduce(stats[:, :, 1], part_max[:], AX.X, ALU.max).then_inc(stats_ready, 1)
                dve.wait_ge(summed, 1 + 10 * b + 10)
                dve.tensor_reduce(stats[:, :, 0], part_sum[:], AX.X, ALU.add).then_inc(stat_steps, 1)
                dve.wait_ge(stat_steps, b + 1)
                dve.tensor_scalar(stats[:, :, 0], stats[:, :, 0], 1.0 / PXS, None, ALU.mult).then_inc(stats_ready, 1)
                dve.wait_ge(mlp1_done, b + 1)
                dve.tensor_scalar(hidden[:], BANK[5][0:HID, 0:2], 0.0, None, ALU.max).then_inc(gate_steps, 1)
                dve.wait_ge(gate_steps, 3 * b + 1)
                dve.tensor_tensor(hidden_sum[:], hidden[:, 0:1], hidden[:, 1:2], ALU.add).then_inc(mlp1_ready, 1)
                dve.wait_ge(gate_exp, b + 1)
                dve.tensor_scalar(chan_gate[:], chan_gate[:], 1.0, None, ALU.add).then_inc(gate_steps, 1)
                dve.wait_ge(gate_steps, 3 * b + 2)
                dve.reciprocal(chan_gate[:], chan_gate[:]).then_inc(gate_steps, 1)
                for t in range(CT):
                    dve.wait_ge(proj_hi_ready, 2 * b + 1 + t)
                    dve.scalar_tensor_tensor(out=p_lo[:, t, :], in0=proj[:, t, :], scalar=chan_gate[:, t:t + 1],
                                             in1=p_hi[:, t, :].bitcast(F32), op0=ALU.mult,
                                             op1=ALU.subtract).then_inc(proj_ready, 1)

                def low_half(i, k):
                    dve.wait_ge(s_hi_ready, b * 20 + 2 * i + k + 1)
                    dve.tensor_tensor(s_lo[k][:], fused[:, :, bass.ds((2 * i + k) * PX, PX)],
                                      s_hi[k][:].bitcast(F32), ALU.subtract).then_inc(s_ready, 1)

                def butterfly(i, k):
                    s = b * 20 + 2 * i + k
                    for n in range(8):
                        dve.wait_ge(comp_used[n], 1 + s + 1)
                    dve.wait_ge(haar_done[1 - k], 1 + b * 10 + i + k)
                    for t in range(CT):
                        for n, op in enumerate((ALU.add, ALU.subtract)):
                            dve.tensor_tensor(pairs[:, t, 2 * n:2 * n + 2, :], comp[k][:, t, 0:3:2, :],
                                              comp[k][:, t, 1:4:2, :], op).then_inc(pairs_ready, 1)
                    dve.wait_ge(out_stored[k], 1 + (b * 10 + i) * 16)
                    for t in range(CT):
                        dve.wait_ge(pairs_ready, 4 * s + 2 * t + 2)
                        for n, op in enumerate((ALU.add, ALU.subtract)):
                            last = dve.tensor_tensor(result[k][:, t, 2 * n:2 * n + 2, :], pairs[:, t, 0:3:2, :],
                                                     pairs[:, t, 1:4:2, :], op)
                    last.then_inc(haar_done[k], 1)

                low_half(0, 0)
                with dve.Fori(0, LAST) as i:
                    for k in range(2):
                        low_half(*after(i, k, 1))
                        butterfly(i, k)
                low_half(LAST, 1)
                butterfly(LAST, 0)
                butterfly(LAST, 1)

        @block.gpsimd
        def _(pool):
            for semaphore in FROM_ONE:
                pool.sem_inc(semaphore, 1)
            with pool.Fori(0, B) as b:
                wait_alone(pool, (haar_done[0], 10 * b), (haar_done[1], 10 * b), (comp_done[7], 20 * b))
                for tile in (early_rows, late_rows):
                    pool.memset(tile[:, :, C:C + 1], 1.0).then_inc(area_reset, 1)

                def shift_rows(i, k):
                    wait_alone(pool, (product_done[k % 2], b * 10 + before(i, k)),
                               (m_row_ready, b * 20 + SLOTS * i + k + 1))
                    pool.tensor_tensor(expo[k % 2][:], x_rows_of(k), m_row[k % 2][:].rearrange(
                        "p (a c) -> p a c", a=1).broadcast_to([P, TILES, C]), ALU.subtract).then_inc(shifted[k % 2], 1)

                over_chunks(pool, shift_rows, S)

                def pick(i, k):
                    pool.tensor_copy(key_max_now[k][:], key_max[:, bass.ds(2 * i + k, 1), :].rearrange(
                        "p s t -> p (s t)")).then_inc(keymax_now, 1)

                def keep(i, k):
                    s = b * 20 + 2 * i + k
                    wait_alone(pool, (conv_used[0], s * 5 + 1), (conv_used[1], s * 5 + 1))
                    pool.tensor_copy(fused[:, :, bass.ds((2 * i + k) * PX, PX)], fused_now[k][:]).then_inc(fused_kept, 1)

                wait_alone(pool, (keymax_ready, b * 20 + 20), (s_ready, b * 20))
                def low_keys(i, k):
                    s = b * 20 + 2 * i + k
                    for n in range(PIECES):
                        wait_alone(pool, (key_hi_ready, s * PIECES + n + 1))
                        pool.tensor_tensor(piece_of(key_lo4, n), piece_of(slot4(k), n),
                                           piece_of(key_hi4, n).bitcast(F32), ALU.subtract).then_inc(keys_ready, 1)

                def chunk(i, k):
                    if is_chunk(*after(i, k, 3)):
                        wait_alone(pool, (spread_used, (b * 20 + 2 * i + k + 2) * PIECES))
                        pick(*after(i, k, 3))
                    if is_chunk(*after(i, k, 2)):
                        low_keys(*after(i, k, 2))
                    keep(i, k)

                for k in range(2):
                    pick(0, k)
                low_keys(0, 0)
                wait_alone(pool, (spread_used, (b * 20 + 1) * PIECES))
                pick(1, 0)
                low_keys(0, 1)
                stage2(pool, chunk)

                with pool.Fori(0, S // 2) as i:
                    for k in range(2):
                        pool.wait_ge(haar_done[k], 1 + b * 10 + i + 1)
                        pool.wait_ge(ring_loaded[k], (b * LOADS + GROUPS + S // 2 + i + 1) * 16)
                        r = result[k][:].rearrange("p t a n -> p (t a n)").rearrange("p (r c) -> p r c", c=C)
                        pool.tensor_tensor(r, slot(k), r, ALU.add).then_inc(added[k], 1)

        @block.scalar
        def _(act):
            act.wait_ge(prep, VAR_READY[0])
            act.activation(small[:, 0:10], small[:, 0:10], ACT.Sqrt).then_inc(prep_root, 1)
            act.wait_ge(prep, PREP_DONE[0])
            with act.Fori(0, B) as b:
                act.activation(unused[:], gam[:], ACT.Exp)
                def scales(i, k):
                    s = b * 20 + SLOTS * i + k
                    act.wait_ge(m_row_done, s + 1)
                    act.wait_ge(shifted[k % 2], 1 + b * 10 + before(i, k))
                    act.activation(m_row[k % 2][:], m_bank[:, 0:C], ACT.Copy).then_inc(m_row_ready, 1)
                    act.wait_ge(max_steps, 2 * s + 2)
                    act.activation(rescale[:, k, :], rescale[:, k, :], ACT.Exp).then_inc(rescale_ready, 1)

                def exponentials(i, k):
                    act.wait_ge(shifted[k % 2], 1 + b * 10 + before(i, k) + 1)
                    act.activation(expo[k % 2][:], expo[k % 2][:], ACT.Exp).then_inc(expo_ready, 1)

                scales(0, 0)
                exponentials(0, 0)
                scales(0, 1)

                def both(i, k):
                    exponentials(*after4(i, k, 1))
                    scales(*after4(i, k, 2))

                over_chunks(act, both, S - 2)
                exponentials(GROUPS - 1, SLOTS - 1)

                def exp_keys(i, k):
                    for n in range(PIECES):
                        act.wait_ge(spread_used, 1 + (b * 20 + 2 * i + k) * PIECES + n + 1)
                        act.activation(piece_of(slot4(k), n), piece_of(slot4(k), n), ACT.Exp).then_inc(keys_exp, 1)

                def high_keys(i, k):
                    s = b * 20 + 2 * i + k
                    for t in range(CT):
                        act.wait_ge(attn_done[t], 1 + s * JC)
                    for n in range(PIECES):
                        act.wait_ge(keys_exp, s * PIECES + n + 1)
                        act.activation(piece_of(key_hi4, n), piece_of(slot4(k), n), ACT.Copy).then_inc(key_hi_ready, 1)

                def evacuate(i, k):
                    s = b * 20 + 2 * i + k
                    for t in range(CT):
                        act.wait_ge(conv_done[t], 1 + s * 5 + 1)
                        act.wait_ge(fused_kept, 1 + s)
                        act.wait_ge(px_done, 1 + 2 * s)
                        act.activation(fused_now[k][:, t, :], conv_bank[t][:, 0:PX], ACT.Relu, bias=bias1[:, t:t + 1],
                                       scale=scale1[:, t:t + 1]).then_inc(conv_used[t], 1)
                    for t in range(CT):
                        act.wait_ge(y_stored[t], 1 + s * 16)
                        for q in range(4):
                            act.wait_ge(conv_done[q % 2], 1 + s * 5 + 2 + 2 * t + q // 2)
                            act.activation(y_out[t][:, q * PX:(q + 1) * PX], conv_bank[q % 2][:, 0:PX], ACT.Identity,
                                           bias=vec[:, VEC["conv_b"] + t:VEC["conv_b"] + t + 1]).then_inc(
                                               conv_used[q % 2], 1)

                def chunk(i, k):
                    if is_chunk(*after(i, k, 2)):
                        high_keys(*after(i, k, 2))
                    evacuate(i, k)
                    if is_chunk(*after(i, k, 3)):
                        exp_keys(*after(i, k, 3))

                exp_keys(0, 0)
                high_keys(0, 0)
                exp_keys(0, 1)
                high_keys(0, 1)
                exp_keys(1, 0)
                stage2(act, chunk)

                act.wait_ge(att_done, b + 1)
                act.activation(sig[:], BANK[4][0:H2, 0:W2], ACT.Exp, scale=-1.0).then_inc(att_exp, 1)
                n = PXS // JC
                for q in range(JC):
                    for t in range(CT):
                        act.wait_ge(gated, 10 * b + 2 * q + t + 1)
                        act.wait_ge(summed, 1 + 10 * b + 2 * q + t)
                        act.activation(junk[:], fused[:, t, q * n:(q + 1) * n], ACT.Copy,
                                       accum_out=part_sum[:, t, q:q + 1]).then_inc(summed, 1)
                act.wait_ge(mlp2_done, b + 1)
                act.activation(chan_gate[:], BANK[6][:, 0:CT], ACT.Exp, scale=-1.0).then_inc(gate_exp, 1)

                act.wait_ge(gate_steps, 3 * b + 3)
                for t in range(CT):
                    act.activation(p_hi[:, t, :], proj[:, t, :], ACT.Copy, scale=chan_gate[:, t:t + 1]).then_inc(
                        proj_hi_ready, 1)

                def high_half(i, k):
                    act.wait_ge(comp_done[7], 1 + (b * 20 if isinstance(i, int) and i == 0 else b * 20 + 2 * i + k - 1))
                    act.activation(s_hi[k][:], fused[:, :, bass.ds((2 * i + k) * PX, PX)], ACT.Copy).then_inc(
                        s_hi_ready, 1)

                def components(i, k):
                    s = b * 20 + 2 * i + k
                    act.wait_ge(haar_done[k], 1 + b * 10 + i)
                    for n in range(8):
                        act.wait_ge(comp_done[n], 1 + s + 1)
                        act.activation(comp[k][:, n % 2, n // 2, :], BANK[n][:, 0:PX], ACT.Relu,
                                       bias=bias2[:, n:n + 1], scale=scale2[:, n:n + 1]).then_inc(comp_used[n], 1)

                high_half(0, 0)
                with act.Fori(0, LAST) as i:
                    for k in range(2):
                        high_half(*after(i, k, 1))
                        components(i, k)
                high_half(LAST, 1)
                components(LAST, 0)
                components(LAST, 1)

        @block.tensor
        def _(pe):
            pe.wait_ge(prep, FQ_READY[0])
            pe.wait_ge(weights_loaded, 144)
            for n in range(4):
                t, q0 = n // 2, n % 2 * 2
                for q in range(2):
                    for m in range(CT):
                        last = pe.matmul(BANK[n][:, q * C:(q + 1) * C], wn[:, m, t * P:(t + 1) * P], fq[:, q0 + q, m, :],
                                         start=(m == 0), stop=(m == CT - 1))
                last.then_inc(prep_mm, 1)
            for t in range(CT):
                for q in range(4):
                    for m in range(CT):
                        last = pe.matmul(BANK[4 + t][:, 0:1], fq[:, q, m, t * P:(t + 1) * P],
                                         vec[:, VEC["conv_b"] + m:VEC["conv_b"] + m + 1],
                                         start=(q == 0 and m == 0), stop=(q == 3 and m == CT - 1))
                last.then_inc(prep_mm, 1)
            pe.wait_ge(prep, PREP_DONE[0])

            with pe.Fori(0, B) as b:
                for n in range(8):
                    pe.wait_ge(comp_used[n], 1 + 20 * b)
                def turn_maxima(i, k):
                    pe.wait_ge(tile_max_ready, b * 20 + SLOTS * i + k + 1)
                    for t in range(CT):
                        last = pe.transpose(turned_bank[:, t * P:(t + 1) * P], tile_max[:, t * P:(t + 1) * P], ident[:])
                    last.then_inc(turned, 1)

                def spread_m(i, k):
                    s = b * 20 + SLOTS * i + k
                    pe.wait_ge(chan_max_ready, s + 1)
                    pe.wait_ge(m_row_ready, 1 + s)
                    for t in range(CT):
                        last = pe.transpose(m_bank[:, t * P:(t + 1) * P],
                                            chan_max[:, k, t:t + 1].broadcast_to([P, P]), ident[:])
                    last.then_inc(m_row_done, 1)

                def spread_maxima(i, k):
                    s = b * 20 + 2 * i + k
                    pe.wait_ge(keymax_now, 1 + s + 1)
                    pe.wait_ge(spread_used, 1 + s * PIECES)
                    if not isinstance(i, int) or 2 * i + k > 1:
                        before_i, before_k = after(i, k, -2)
                        for h in range(CT):
                            pe.wait_ge(attn_used[1][h], 1 + (b * 10 + before_i) * JC + blocks_after(before_k, 1))
                    for j in range(JC):
                        for h in range(CT):
                            n = (j % 2) * C + h * P
                            last = pe.transpose(max_bank[j // 2][:, n:n + P],
                                                key_max_now[k][:, h * JC + j:h * JC + j + 1].broadcast_to([P, P]), ident[:])
                        if j % 2 or j == JC - 1:
                            last.then_inc(spread, 1)

                def product_tiles(k, first, end):
                    for r in range(first, end):
                        for t in range(CT):
                            last = pe.matmul(chunk_bank[k % 2][t][:, 0:C + 1], expo[k % 2][:, r, t * P:(t + 1) * P],
                                             rows[k][:, r, :], start=(r == 0), stop=(r == TILES - 1))
                    return last

                def accumulate(i, k):
                    pe.wait_ge(expo_ready, b * 20 + SLOTS * i + k + 1)
                    pe.wait_ge(merged[k % 2], 1 + CT * (b * 10 + before(i, k)))
                    if isinstance(i, int) and i == GROUPS - 1 and k >= SLOTS - 2:
                        product_tiles(k, 0, TILES - 2)
                        if k == SLOTS - 1:
                            spread_maxima(0, 1)
                        last = product_tiles(k, TILES - 2, TILES)
                    else:
                        product_tiles(k, 0, TILES // 2)
                        turn_maxima(*after4(i, k, 2))
                        product_tiles(k, TILES // 2, TILES - 1)
                        spread_m(*after4(i, k, 2))
                        last = product_tiles(k, TILES - 1, TILES)
                    last.then_inc(product_done[k % 2], 1)

                for k in range(2):
                    turn_maxima(0, k)
                    spread_m(0, k)
                wait_alone(pe, (area_reset, 2 * b + 2))
                over_chunks(pe, accumulate, S - 2)
                accumulate(GROUPS - 1, SLOTS - 2)
                wait_alone(pe, (m_row_ready, 20 * b + 20))
                spread_maxima(0, 0)
                accumulate(GROUPS - 1, SLOTS - 1)

                def product(dst, pairs_, done):
                    n = 0
                    for (a_hi, a_lo), (x_hi, x_lo) in pairs_:
                        for a, x in ((a_hi, x_hi), (a_hi, x_lo), (a_lo, x_hi)):
                            last = pe.matmul(dst, a, x, start=(n == 0), stop=(n == 3 * len(pairs_) - 1))
                            n += 1
                    last.then_inc(done, 1)

                def attend(i, k):
                    s = b * 20 + 2 * i + k
                    pe.wait_ge(spread_used, 1 + (s + (2 if is_chunk(*after(i, k, 1)) else 1)) * PIECES)
                    for j in range(JC):
                        n = (k + j) % 2
                        if j % 2 == 0:
                            pe.wait_ge(keys_ready, s * PIECES + j // 2 + 1)
                        for h in range(CT):
                            pe.wait_ge(attn_used[n][h], 1 + (b * 10 + i) * JC + blocks_before(k, j))
                            product(acc[n][:, h, 0:C + 2],
                                    [((key_hi[:, t * JC + j, h * P:(h + 1) * P],
                                       key_lo[:, t * JC + j, h * P:(h + 1) * P]),
                                      (vq_hi[:, t, :], vq_lo[:, t, :])) for t in range(CT)], attn_done[h])

                def fuse(i, k):
                    s = b * 20 + 2 * i + k
                    pe.wait_ge(split_ready, 1 + s + 1)
                    for m in range(CT):
                        pe.wait_ge(conv_used[m], 1 + s * 5)
                        cols = slice(m * P, (m + 1) * P)
                        product(conv_bank[m][:, 0:PX],
                                [((g_hi[:, t, q, cols], g_lo[:, t, q, cols]),
                                  (parity(o_hi[k], t, q), parity(o_lo[k], t, q))) for q in range(4) for t in range(CT)],
                                conv_done[m])

                def convolve(i, k, m):
                    s = b * 20 + 2 * i + k
                    cols = slice(m * P, (m + 1) * P)
                    for n in range(4):
                        q = n % 2 * 2 + n // 2
                        pe.wait_ge(conv_used[n % 2], 1 + s * 5 + 1 + 2 * m + n // 2)
                        product(conv_bank[n % 2][:, 0:PX],
                                [((w_hi[:, t, cols], w_lo[:, t, cols]),
                                  (parity(o_hi[k], t, q), parity(o_lo[k], t, q))) for t in range(CT)],
                                conv_done[n % 2])

                def turn(i, k, n):
                    s = b * 20 + 2 * i + k
                    for t in range(CT):
                        pe.wait_ge(conv_used[t], 1 + s * 5 + 1)
                    pe.wait_ge(px_used, 1 + 2 * s + n)
                    for r in range(2):
                        for t in range(CT):
                            px = (2 * n + r) * W2
                            last = pe.transpose(px_bank[0:W2, r * C + t * P:r * C + (t + 1) * P],
                                                fused_now[k][:, t, px:px + W2], ident[:])
                    last.then_inc(px_done, 1)

                def chunk(i, k):
                    if is_chunk(*after(i, k, 1)):
                        attend(*after(i, k, 1))
                    fuse(i, k)
                    convolve(i, k, 0)
                    turn(i, k, 0)
                    if is_chunk(*after(i, k, 3)):
                        spread_maxima(*after(i, k, 3))
                    convolve(i, k, 1)
                    turn(i, k, 1)

                pe.wait_ge(vq_scaled, 2 * b + 2)
                for t in range(CT):
                    for d in range(CT):
                        last = pe.transpose(conv_bank[t][:, d * P:(d + 1) * P], vqT[:, d, t * P:(t + 1) * P], ident[:])
                last.then_inc(vq_turned, 1)
                pe.wait_ge(vq_ready, 2 * b + 2)
                attend(0, 0)
                spread_maxima(1, 0)
                stage2(pe, chunk)

                pe.wait_ge(maps_ready, b + 1)
                for m in range(2):
                    for ky in range(KS):
                        last = pe.matmul(BANK[4][0:H2, 0:W2], maps[:, m, ky:ky + H2], band[:, m * KS + ky, :],
                                         start=(m == 0 and ky == 0), stop=(m == 1 and ky == KS - 1))
                last.then_inc(att_done, 1)
                pe.wait_ge(stats_ready, 2 * b + 2)
                for t in range(CT):
                    last = pe.matmul(BANK[5][0:HID, 0:2], w1[:, t, :], stats[:, t, :], start=(t == 0), stop=(t == CT - 1))
                last.then_inc(mlp1_done, 1)
                pe.wait_ge(mlp1_ready, b + 1)
                for t in range(CT):
                    last = pe.matmul(BANK[6][:, t:t + 1], w2[:, t * P:(t + 1) * P], hidden_sum[:], start=True, stop=True)
                last.then_inc(mlp2_done, 1)

                wait_alone(pe, (gate_exp, b + 1), (proj_ready, 2 * b + 2))
                wait_alone(pe, (conv_used[0], 100 * b + 100), (conv_used[1], 100 * b + 100))
                with pe.Fori(0, S // 2) as i:
                    for k in range(2):
                        s = b * 20 + 2 * i + k
                        pe.wait_ge(s_ready, 1 + s + 1)
                        for n in range(8):
                            pe.wait_ge(comp_used[n], 1 + s)
                            cols = slice(n * P, (n + 1) * P)
                            for m, (a, x) in enumerate((a, x) for t in range(CT) for a, x in (
                                    (p_hi[:, t, cols], s_hi[k][:, t, :]), (p_hi[:, t, cols], s_lo[k][:, t, :]),
                                    (p_lo[:, t, cols], s_hi[k][:, t, :]))):
                                last = pe.matmul(BANK[n][:, 0:PX], a, x, start=(m == 0), stop=(m == 5))
                            last.then_inc(comp_done[n], 1)


def kernel(x, L0_conv_conv_w, L0_conv_conv_b, L0_conv_gamma, L1_conv_fusion_w, L1_conv_fusion_b, L1_conv_bn1_g,
           L1_conv_bn1_b, L1_conv_bn1_m, L1_conv_bn1_v, L1_conv_sa_w, L1_conv_ca_w1, L1_conv_ca_w2, L1_conv_proj_w,
           L1_conv_proj_b, L1_conv_bn2_g, L1_conv_bn2_b, L1_conv_bn2_m, L1_conv_bn2_v):
    import concourse.bacc as bacc
    from concourse.bass_utils import run_bass_kernel_spmd

    x = np.asarray(x)
    B = x.shape[0]
    blocks = x.reshape(B, CT, P, CT, P, S, JC)
    x_rows = np.zeros((B * S + 2, P, CT * POS), x.dtype)
    x_rows[:B * S] = blocks.transpose(0, 5, 4, 3, 6, 1, 2).reshape(B * S, P, CT * POS)
    x_keys = blocks.transpose(0, 5, 2, 1, 6, 3, 4).reshape(B, S, P, CT * POS)
    x_pos = x.reshape(B, CT, P, S, ROWS, W2, 2).transpose(0, 3, 2, 1, 6, 4, 5).reshape(B, S, P, CT * POS)

    def columns(v):
        return np.asarray(v).reshape(-1, P).T

    vectors = np.concatenate([columns(v) for v in (
        L0_conv_conv_b, L1_conv_fusion_b, L1_conv_bn1_g, L1_conv_bn1_b, L1_conv_bn1_m, L1_conv_bn1_v, L1_conv_proj_b,
        L1_conv_bn2_g, L1_conv_bn2_b, L1_conv_bn2_m, L1_conv_bn2_v)], axis=1)
    sa = np.asarray(L1_conv_sa_w)[0]
    bands = np.zeros((W2, 2 * KS, W2), sa.dtype)
    for m in range(2):
        for ky in range(KS):
            for w_out in range(W2):
                for kx in range(KS):
                    w_in = w_out + kx - PAD
                    if 0 <= w_in < W2:
                        bands[w_in, m * KS + ky, w_out] = sa[m, ky, kx]

    arrays = {
        "x_rows": x_rows, "x_keys": x_keys, "x_pos": x_pos, "conv_w": np.asarray(L0_conv_conv_w),
        "conv_wT": np.asarray(L0_conv_conv_w).T, "fusion_wT": np.asarray(L1_conv_fusion_w).T,
        "proj_wT": np.asarray(L1_conv_proj_w).T, "w1T": np.asarray(L1_conv_ca_w1).T,
        "w2T": np.asarray(L1_conv_ca_w2).T, "vectors": vectors, "gamma": np.asarray(L0_conv_gamma), "bands": bands,
        "identity": np.eye(P, dtype=np.float32),
    }
    arrays = {f"in_{k}": np.ascontiguousarray(v) for k, v in arrays.items()}
    nc = bacc.Bacc("TRN2", target_bir_lowering=False, num_devices=1)
    args = [nc.dram_tensor(k, v.shape, mybir.dt.from_np(v.dtype), kind="ExternalInput").ap() for k, v in arrays.items()]
    out = nc.dram_tensor("out", (B, S, P, CT * POS), F32, kind="ExternalOutput").ap()
    build(nc, B, *args, out)
    got = run_bass_kernel_spmd(nc, [arrays], core_ids=[0]).results[0]["out"]
    return np.ascontiguousarray(got.reshape(B, S, P, CT, 2, 2, HR, W2).transpose(0, 3, 2, 1, 6, 5, 7, 4)).reshape(B, C, H, W)
```
